# Optimizing a Trainium2 kernel written in Bass

```python
import numpy as np
import jax
import jax.numpy as jnp

def _softmax(x, axis=-1):
    return jax.nn.softmax(x, axis=axis)

def _gelu(x):
    return jax.nn.gelu(x, approximate=True)

def _silu(x):
    return jax.nn.silu(x)

def _sigmoid(x):
    return jax.nn.sigmoid(x)

def _layernorm(x, axis=-1, eps=1e-05):
    m = jnp.mean(x, axis=axis, keepdims=True)
    v = jnp.var(x, axis=axis, keepdims=True)
    return (x - m) / jnp.sqrt(v + eps)

def _scatter_add(tgt, idx, src, axis=0):
    return tgt.at[idx].add(src)

def _segment_sum(src, seg, n):
    return jax.ops.segment_sum(src, seg, n)
kernel_name = 'mk_lm_tower_d1_tok_ids1024_r4_73f45f'

def setup_inputs(seed: int=0):
    np.random.seed(seed)
    _w = jnp.asarray

    def _rec_inputs():
        import jax
        import jax.numpy as jnp
        _rk = jax.random.key(seed)
        x = jax.random.randint(jax.random.fold_in(_rk, 1), (1, 2048), 0, 12500, jnp.int32)
        return x
    x = _rec_inputs()

    def _L0_tok_setup():
        import jax, jax.numpy as jnp
        import numpy as np
        VOCAB = 12500
        EMBED_DIM = 256
        HALF = EMBED_DIM // 2
        BATCH, SEQ = (32, 512)
        key = jax.random.key(seed)
        ks = jax.random.split(key, 7)
        token_ids = jax.random.randint(ks[0], (BATCH, SEQ), 0, VOCAB)
        token_table = jax.random.normal(ks[1], (VOCAB, HALF), dtype=jnp.float32)
        op_table = jax.random.normal(ks[2], (10, HALF), dtype=jnp.float32)
        var_table = jax.random.normal(ks[3], (10, HALF), dtype=jnp.float32)
        const_table = jax.random.normal(ks[4], (10, HALF), dtype=jnp.float32)
        struct_table = jax.random.normal(ks[5], (10, HALF), dtype=jnp.float32)
        special_table = jax.random.normal(ks[6], (VOCAB - 40, HALF), dtype=jnp.float32)
        return {'token_ids': token_ids, 'token_table': token_table, 'op_table': op_table, 'var_table': var_table, 'const_table': const_table, 'struct_table': struct_table, 'special_table': special_table}
    _L0_tok_all = _L0_tok_setup()
    _L0_tok_in = {k: v for k, v in _L0_tok_all.items() if k in ('token_table', 'op_table', 'var_table', 'const_table', 'struct_table', 'special_table')}
    del _L0_tok_all

    def _L0_attn_setup():
        import jax, jax.numpy as jnp
        import numpy as np
        import math
        N_HEAD = 16
        HEAD_DIM = 64
        N_EMBD = 256
        EPS_RMS = 1e-05
        U_L2_EPS = 1e-06

        def _get_alibi_slopes(n_heads):

            def pow2(n):
                start = 2 ** (-2 ** (-(math.log2(n) - 3)))
                return [start * start ** i for i in range(n)]
            if math.log2(n_heads).is_integer():
                return pow2(n_heads)
            c = 2 ** math.floor(math.log2(n_heads))
            s = pow2(c)
            extra = _get_alibi_slopes(2 * c)
            return s + extra[0::2][:n_heads - c]

        def _rmsnorm(x, w):
            var = jnp.mean(jnp.square(x), axis=-1, keepdims=True)
            return x * jax.lax.rsqrt(var + EPS_RMS) * w
        key = jax.random.key(seed)
        ks = jax.random.split(key, 9)
        B, T = (2, 512)
        H, D, C = (N_HEAD, HEAD_DIM, N_EMBD)
        x = jax.random.normal(ks[0], (B, T, C), dtype=jnp.float32)
        sc = 1.0 / math.sqrt(C)
        Wq = jax.random.normal(ks[1], (C, H * D), dtype=jnp.float32) * sc
        Wk = jax.random.normal(ks[2], (C, H * D), dtype=jnp.float32) * sc
        Wv = jax.random.normal(ks[3], (C, H * D), dtype=jnp.float32) * sc
        Wproj = jax.random.normal(ks[4], (H * D, C), dtype=jnp.float32) * (0.5 / math.sqrt(C) / math.sqrt(12))
        q_rms_w = jnp.ones((D,), dtype=jnp.float32)
        k_rms_w = jnp.ones((D,), dtype=jnp.float32)
        omega = jnp.full((H,), math.log(math.expm1(1.0)), dtype=jnp.float32)
        u = jax.random.normal(ks[5], (H, D), dtype=jnp.float32) * (1.0 / math.sqrt(D))
        return {'x': x, 'Wq': Wq, 'Wk': Wk, 'Wv': Wv, 'Wproj': Wproj, 'q_rms_w': q_rms_w, 'k_rms_w': k_rms_w, 'omega': omega, 'u': u}
    _L0_attn_all = _L0_attn_setup()
    _L0_attn_in = {k: v for k, v in _L0_attn_all.items() if k in ('Wq', 'Wk', 'Wv', 'Wproj', 'q_rms_w', 'k_rms_w', 'omega', 'u')}
    del _L0_attn_all

    def _L0_ffn_setup():
        import jax, jax.numpy as jnp
        import numpy as np
        B, S, DIM = (4, 1024, 256)
        BASE_COUPLING = 0.1
        NUM_CYCLES = 3

        def _gelu(x):
            return jax.nn.gelu(x, approximate=False)

        def _coupling_net(h, w1, b1, w2, b2, w3, b3, w4, b4):
            h = _gelu(h @ w1 + b1)
            h = _gelu(h @ w2 + b2)
            h = _gelu(h @ w3 + b3)
            return jax.nn.sigmoid(h @ w4 + b4)

        def _global_net(h, w1, b1, w2, b2, w3, b3):
            h = _gelu(h @ w1 + b1)
            h = _gelu(h @ w2 + b2)
            return jax.nn.sigmoid(h @ w3 + b3)

        def _twist(x):
            o_r, o_i, p_r, p_i = jnp.split(x, 4, axis=-1)
            return jnp.concatenate([p_r, -p_i, -o_r, o_i], axis=-1)
        key = jax.random.key(seed)
        ks = jax.random.split(key, 9)
        d = DIM

        def w(k, fan_in, fan_out):
            return jax.random.normal(k, (fan_in, fan_out), dtype=jnp.float32) / np.sqrt(fan_in).astype(np.float32)
        inp = {'x': jax.random.normal(ks[0], (B, S, d), dtype=jnp.float32)}
        cn_dims = [(d, d), (d, d // 2), (d // 2, d // 4), (d // 4, 1)]
        for i, (a, b) in enumerate(cn_dims):
            inp[f'cn_w{i + 1}'] = w(ks[1 + i], a, b)
            inp[f'cn_b{i + 1}'] = jnp.zeros((b,), dtype=jnp.float32)
        gc_dims = [(d, d // 2), (d // 2, d // 4), (d // 4, 1)]
        for i, (a, b) in enumerate(gc_dims):
            inp[f'gc_w{i + 1}'] = w(ks[5 + i], a, b)
            inp[f'gc_b{i + 1}'] = jnp.zeros((b,), dtype=jnp.float32)
        inp['adaptive_range'] = jnp.full((1,), 0.2, dtype=jnp.float32)
        return inp
    _L0_ffn_all = _L0_ffn_setup()
    _L0_ffn_in = {k: v for k, v in _L0_ffn_all.items() if k in ('cn_w1', 'cn_b1', 'cn_w2', 'cn_b2', 'cn_w3', 'cn_b3', 'cn_w4', 'cn_b4', 'gc_w1', 'gc_b1', 'gc_w2', 'gc_b2', 'gc_w3', 'gc_b3', 'adaptive_range')}
    del _L0_ffn_all
    return {'x': x, 'L0_tok_token_table': _L0_tok_in['token_table'], 'L0_tok_op_table': _L0_tok_in['op_table'], 'L0_tok_var_table': _L0_tok_in['var_table'], 'L0_tok_const_table': _L0_tok_in['const_table'], 'L0_tok_struct_table': _L0_tok_in['struct_table'], 'L0_tok_special_table': _L0_tok_in['special_table'], 'L0_attn_Wq': _L0_attn_in['Wq'], 'L0_attn_Wk': _L0_attn_in['Wk'], 'L0_attn_Wv': _L0_attn_in['Wv'], 'L0_attn_Wproj': _L0_attn_in['Wproj'], 'L0_attn_q_rms_w': _L0_attn_in['q_rms_w'], 'L0_attn_k_rms_w': _L0_attn_in['k_rms_w'], 'L0_attn_omega': _L0_attn_in['omega'], 'L0_attn_u': _L0_attn_in['u'], 'L0_ffn_cn_w1': _L0_ffn_in['cn_w1'], 'L0_ffn_cn_b1': _L0_ffn_in['cn_b1'], 'L0_ffn_cn_w2': _L0_ffn_in['cn_w2'], 'L0_ffn_cn_b2': _L0_ffn_in['cn_b2'], 'L0_ffn_cn_w3': _L0_ffn_in['cn_w3'], 'L0_ffn_cn_b3': _L0_ffn_in['cn_b3'], 'L0_ffn_cn_w4': _L0_ffn_in['cn_w4'], 'L0_ffn_cn_b4': _L0_ffn_in['cn_b4'], 'L0_ffn_gc_w1': _L0_ffn_in['gc_w1'], 'L0_ffn_gc_b1': _L0_ffn_in['gc_b1'], 'L0_ffn_gc_w2': _L0_ffn_in['gc_w2'], 'L0_ffn_gc_b2': _L0_ffn_in['gc_b2'], 'L0_ffn_gc_w3': _L0_ffn_in['gc_w3'], 'L0_ffn_gc_b3': _L0_ffn_in['gc_b3'], 'L0_ffn_adaptive_range': _L0_ffn_in['adaptive_range']}

def reference(x, L0_tok_token_table, L0_tok_op_table, L0_tok_var_table, L0_tok_const_table, L0_tok_struct_table, L0_tok_special_table, L0_attn_Wq, L0_attn_Wk, L0_attn_Wv, L0_attn_Wproj, L0_attn_q_rms_w, L0_attn_k_rms_w, L0_attn_omega, L0_attn_u, L0_ffn_cn_w1, L0_ffn_cn_b1, L0_ffn_cn_w2, L0_ffn_cn_b2, L0_ffn_cn_w3, L0_ffn_cn_b3, L0_ffn_cn_w4, L0_ffn_cn_b4, L0_ffn_gc_w1, L0_ffn_gc_b1, L0_ffn_gc_w2, L0_ffn_gc_b2, L0_ffn_gc_w3, L0_ffn_gc_b3, L0_ffn_adaptive_range):
    import jax
    import jax.numpy as jnp

    def _L0_tok_ref(token_ids, token_table, op_table, var_table, const_table, struct_table, special_table):
        import jax, jax.numpy as jnp
        import numpy as np
        VOCAB = 12500
        EMBED_DIM = 256
        HALF = EMBED_DIM // 2
        BATCH, SEQ = (32, 512)
        token_embeds = token_table[token_ids]
        cat_table = jnp.concatenate([op_table, var_table, const_table, struct_table, special_table], axis=0)
        category_embeds = cat_table[token_ids]
        return jnp.concatenate([token_embeds, category_embeds], axis=-1)

    def _L0_attn_ref(x, Wq, Wk, Wv, Wproj, q_rms_w, k_rms_w, omega, u):
        import jax, jax.numpy as jnp
        import numpy as np
        import math
        N_HEAD = 16
        HEAD_DIM = 64
        N_EMBD = 256
        EPS_RMS = 1e-05
        U_L2_EPS = 1e-06

        def _get_alibi_slopes(n_heads):

            def pow2(n):
                start = 2 ** (-2 ** (-(math.log2(n) - 3)))
                return [start * start ** i for i in range(n)]
            if math.log2(n_heads).is_integer():
                return pow2(n_heads)
            c = 2 ** math.floor(math.log2(n_heads))
            s = pow2(c)
            extra = _get_alibi_slopes(2 * c)
            return s + extra[0::2][:n_heads - c]

        def _rmsnorm(x, w):
            var = jnp.mean(jnp.square(x), axis=-1, keepdims=True)
            return x * jax.lax.rsqrt(var + EPS_RMS) * w
        B, T, C = x.shape
        H, D = (N_HEAD, HEAD_DIM)
        q = (x @ Wq).reshape(B, T, H, D)
        k = (x @ Wk).reshape(B, T, H, D)
        v = (x @ Wv).reshape(B, T, H, D)
        q = _rmsnorm(q, q_rms_w)
        k = _rmsnorm(k, k_rms_w)
        slopes = jnp.asarray(_get_alibi_slopes(H), dtype=jnp.float32)
        omega_eff = jax.nn.softplus(omega) * slopes
        u_n = u / jnp.maximum(jnp.linalg.norm(u, axis=-1, keepdims=True), U_L2_EPS)
        gate_logits = jnp.einsum('bthd,hd->bht', k, u_n) / math.sqrt(D)
        gate = jax.nn.softplus(gate_logits)
        idx = jnp.arange(T)
        dist = jnp.maximum(idx[:, None] - idx[None, :], 0).astype(jnp.float32)
        bias = -dist[None, None] * omega_eff[None, :, None, None] * gate[:, :, None, :]
        causal = idx[:, None] >= idx[None, :]
        bias = jnp.where(causal[None, None], bias, -jnp.inf)
        scale = 1.0 / math.sqrt(D)
        scores = jnp.einsum('bihd,bjhd->bhij', q, k) * scale + bias
        attn = jax.nn.softmax(scores, axis=-1)
        y = jnp.einsum('bhij,bjhd->bihd', attn, v).reshape(B, T, H * D)
        return y @ Wproj

    def _L0_ffn_ref(x, cn_w1, cn_b1, cn_w2, cn_b2, cn_w3, cn_b3, cn_w4, cn_b4, gc_w1, gc_b1, gc_w2, gc_b2, gc_w3, gc_b3, adaptive_range):
        import jax, jax.numpy as jnp
        import numpy as np
        B, S, DIM = (4, 1024, 256)
        BASE_COUPLING = 0.1
        NUM_CYCLES = 3

        def _gelu(x):
            return jax.nn.gelu(x, approximate=False)

        def _coupling_net(h, w1, b1, w2, b2, w3, b3, w4, b4):
            h = _gelu(h @ w1 + b1)
            h = _gelu(h @ w2 + b2)
            h = _gelu(h @ w3 + b3)
            return jax.nn.sigmoid(h @ w4 + b4)

        def _global_net(h, w1, b1, w2, b2, w3, b3):
            h = _gelu(h @ w1 + b1)
            h = _gelu(h @ w2 + b2)
            return jax.nn.sigmoid(h @ w3 + b3)

        def _twist(x):
            o_r, o_i, p_r, p_i = jnp.split(x, 4, axis=-1)
            return jnp.concatenate([p_r, -p_i, -o_r, o_i], axis=-1)
        global_context = x.mean(axis=1, keepdims=True)
        gf = _global_net(global_context, gc_w1, gc_b1, gc_w2, gc_b2, gc_w3, gc_b3)
        out = x
        for _ in range(NUM_CYCLES):
            tf = _coupling_net(out, cn_w1, cn_b1, cn_w2, cn_b2, cn_w3, cn_b3, cn_w4, cn_b4)
            combined = 0.7 * gf + 0.3 * tf
            coupling = BASE_COUPLING + adaptive_range * (combined - 0.5) * 2.0
            out = out + coupling * _twist(out)
        return out
    h = _L0_tok_ref(x, L0_tok_token_table, L0_tok_op_table, L0_tok_var_table, L0_tok_const_table, L0_tok_struct_table, L0_tok_special_table)
    h = h + _L0_attn_ref(_layernorm(h, axis=-1), L0_attn_Wq, L0_attn_Wk, L0_attn_Wv, L0_attn_Wproj, L0_attn_q_rms_w, L0_attn_k_rms_w, L0_attn_omega, L0_attn_u)
    h = h + _L0_ffn_ref(_layernorm(h, axis=-1), L0_ffn_cn_w1, L0_ffn_cn_b1, L0_ffn_cn_w2, L0_ffn_cn_b2, L0_ffn_cn_w3, L0_ffn_cn_b3, L0_ffn_cn_w4, L0_ffn_cn_b4, L0_ffn_gc_w1, L0_ffn_gc_b1, L0_ffn_gc_w2, L0_ffn_gc_b2, L0_ffn_gc_w3, L0_ffn_gc_b3, L0_ffn_adaptive_range)
    return h

_drawn_inputs = setup_inputs


def setup_inputs(seed=0):
    import zlib

    import numpy as np

    out = dict(_drawn_inputs(seed))
    spreads = {'L0_attn_q_rms_w': (1.0, 0.6),
     'L0_attn_k_rms_w': (1.0, 0.6),
     'L0_attn_omega': (0.5413248538970947, 0.6),
     'L0_ffn_cn_b1': (0.0, 2.0),
     'L0_ffn_cn_b2': (0.0, 2.0),
     'L0_ffn_cn_b3': (0.0, 2.0),
     'L0_ffn_gc_b1': (0.0, 2.0),
     'L0_ffn_gc_b2': (0.0, 0.8)}
    factors = {'L0_tok_op_table': 2.766,
     'L0_attn_u': 36.077,
     'L0_ffn_cn_w1': 7.234,
     'L0_ffn_cn_w2': 7.492,
     'L0_ffn_cn_w3': 5.992,
     'L0_ffn_cn_w4': 6.901,
     'L0_ffn_gc_w1': 64.0,
     'L0_ffn_gc_w2': 64.0,
     'L0_ffn_gc_w3': 5.609}
    for name, (base, spread) in spreads.items():
        noise = np.random.default_rng([zlib.crc32(name.encode()), seed]).standard_normal(out[name].shape)
        drawn = base * np.exp(spread * noise) if base else spread * noise
        out[name] = jnp.asarray(drawn.astype(out[name].dtype))
    for name, factor in factors.items():
        out[name] = (out[name] * factor).astype(out[name].dtype)
    return out
```

```python
import concourse.bass as bass
from concourse import mybir
from contextlib import ExitStack

F32 = mybir.dt.float32
F32R = mybir.dt.float32r
F16 = mybir.dt.float16
BF16 = mybir.dt.bfloat16
I32 = mybir.dt.int32
U32 = mybir.dt.uint32
ALU = mybir.AluOpType
ACT = mybir.ActivationFunctionType
AX = mybir.AxisListType

T = 2048
HALF = 128
C = 256
H = 16
D = 64
P = 128
NT = T // P
NP = H // 2
BLK = 512
NB = T // BLK
TPB = BLK // P
SMALL = 10
NSMALL = 4 * SMALL
CYCLES = 3
FF_LOADS = 16
EXP_LN_SET = "natural_log_exp_and_others"
EPS = 1e-5
U_EPS = 1e-6
NEG = -1e30
FAR = 1e6
NC = 5
MAX_ROW = P - 1
S_RING, MX_RING, P_RING = 3, 2, 10


def at_least(eng, sem, value):
    if isinstance(value, int) and value <= 0:
        return
    eng.wait_ge(sem, value)


def block_tiles(b):
    return TPB * (b + 1)


BIAS_AT = [sum(block_tiles(x) for x in range(b)) for b in range(NB)]
STEPS = [(b, j) for b in range(NB) for j in range(block_tiles(b))]
NSTEP = len(STEPS)
MAXES = [(b, q, hd, ch) for b in range(NB) for q in range(TPB) for hd in range(2) for ch in range(b + 1)]
NMAX = len(MAXES)
MAX_END = [sum(m[0] <= b for m in MAXES) for b in range(NB)]
LEAD = NMAX - 2 * (NSTEP // 2)


def tower(nc, x, tok_table, op_table, var_table, const_table, struct_table, special_table,
          wq, wk, wv, wproj, q_w, k_w, omega, u,
          cn_w1, cn_b1, cn_w2, cn_b2, cn_w3, cn_b3, cn_w4, cn_b4,
          gc_w1, gc_b1, gc_w2, gc_b2, gc_w3, gc_b3, ada, out):
    nc.disable_value_cache = True
    ctx = ExitStack()
    with ctx:
        def sb(name, shape, dt, where=ctx):
            return where.enter_context(nc.sbuf_tensor(name, shape, dt))

        def sem(name):
            return ctx.enter_context(nc.semaphore(name))

        small_d = nc.dram_tensor("small_d", [NSMALL, HALF], F32).ap()
        qT_d = nc.dram_tensor("qT_d", [H, P, T], F16).ap()
        kT_d = nc.dram_tensor("kT_d", [H, P, T], F16).ap()
        v_d = nc.dram_tensor("v_d", [T, H * D], F32).ap()
        c_d = nc.dram_tensor("c_d", [NC * H, T], F16).ap()

        E = sb("E", [P, NT, C], F32)
        ident = sb("ident", [P, P], F32)
        ident16 = sb("ident16", [P, P], F16)
        identb = sb("identb", [P, P], BF16)
        mask_s = sb("mask_s", [P, P], BF16)
        mask_m = sb("mask_m", [P, P], BF16)
        eps_t = sb("eps_t", [P, 1], F32)
        slope = sb("slope", [P, H], F32)
        off_i = sb("off_i", [P, NSTEP], I32)
        off = sb("off", [P, NSTEP], F32)
        BT = sb("BT", [P, H, NSTEP], F32)
        A1 = sb("A1", [P, 2, 2, T], F16)
        B1 = sb("B1", [P, 2, T], F16)
        BM = sb("BM", [P, 2, T], F16)
        wp = sb("wp", [P, NP, C], F32)

        pre = ExitStack()
        ids = sb("ids", [P, NT], I32, pre)
        far = sb("far", [P, NT], F32, pre)
        spec_ids = sb("spec_ids", [P, NT], I32, pre)
        wst = sb("wst", [P, 2, H * D], F32, pre)
        wh = sb("wh", [P, 2, 3, H * D], F32R, pre)
        wl = sb("wl", [P, 2, 3, H * D], F32R, pre)
        wgf = sb("wgf", [P, 2, H], F32, pre)
        wgh = sb("wgh", [P, 2, H], F32R, pre)
        wgl = sb("wgl", [P, 2, H], F32R, pre)
        ub = sb("ub", [P, H, D], F32, pre)
        tmp = sb("tmp", [P, H, D], F32, pre)
        qwb = sb("qwb", [P, D], F32, pre)
        kwb = sb("kwb", [P, D], F32, pre)
        wqk = sb("wqk", [P, D], F32, pre)
        un = sb("un", [P, H], F32, pre)
        bn6 = sb("bn6", [P, 2, 6], F32, pre)
        mv = sb("mv", [P, 2, 2], F32, pre)
        ls = sb("ls", [P, 2, 1], F32, pre)
        lr = sb("lr", [P, 2, 1], F32, pre)
        XN = sb("XN", [P, 2, C], F32, pre)
        XH = sb("XH", [P, 2, 2, P], F32R, pre)
        XL = sb("XL", [P, 2, 2, P], F32R, pre)
        SQ = sb("SQ", [P, 2 * H, D], F32, pre)
        ms = sb("ms", [P, 2 * H], F32, pre)
        sr = sb("sr", [P, 2 * H], F32, pre)
        rr = sb("rr", [P, 2 * H], F32, pre)
        QN = sb("QN", [P, H, D], F32, pre)
        KN = sb("KN", [P, H, D], F32, pre)
        KW = sb("KW", [P, H, D], F32, pre)
        QT = sb("QT", [P, 2, H, P], F16, pre)
        KT = sb("KT", [P, 2, H, P], F16, pre)
        VS = sb("VS", [P, 2, H * D], F32, pre)
        STQ = sb("STQ", [P, H, 2 * P], F16, pre)
        STK = sb("STK", [P, H, 2 * P], F16, pre)
        GL = sb("GL", [P, NT + 1, H], F32, pre)
        na = sb("na", [P, NT + 1, H], F32, pre)
        sp = sb("sp", [P, NT + 1, H], F32, pre)
        cw = sb("cw", [P, H], F32, pre)
        cc = sb("cc", [P, NT, H], F32, pre)
        rest = sb("rest", [P, NT, H], F32, pre)
        CP = sb("CP", [P, NT, H, NC], F16, pre)
        jc = sb("jc", [P, NT, H], F32, pre)
        at_j = sb("at_j", [P, NT], F32, pre)
        CT = sb("CT", [NC * H, T], F16, pre)
        pre.close()

        OT = sb("OT", [P, NP, T], F32)
        att = ExitStack()
        A2 = sb("A2", [P, 2, T], F16, att)
        B2 = sb("B2", [P, 2, T], F16, att)
        V = sb("V", [P, NT, P], F32, att)
        PB = sb("PB", [P, P_RING, BLK], F32, att)
        acc = sb("acc", [P, 2, 2, BLK], F32, att)
        lnr = sb("lnr", [P, BLK], F32, att)
        R = sb("R", [P, BLK], F32, att)
        bts = sb("bts", [P, 2, 2, NSTEP], F32, att)
        mxp = sb("mxp", [P, 2, NB, 2 * TPB, NB], F32, att)
        nmf = sb("nmf", [P, 2, TPB, 2], F32, att)
        nm = sb("nm", [P, 2, 2, TPB], F16, att)
        mrow = sb("mrow", [2 * 2 * TPB, P], F16, att)
        ones = sb("ones", [P, D], F32, att)
        att.close()

        TT = sb("TT", [P, 2, T], F32)
        X2 = sb("X2", [P, 2, C], F32)
        bn6b = sb("bn6b", [P, 2, 6], F32)
        mvb = sb("mvb", [P, 2, 2], F32)
        lsb = sb("lsb", [P, 2, 1], F32)
        lrb = sb("lrb", [P, 2, 1], F32)
        gm = sb("gm", [P, 2, NT], F32)
        gmean = sb("gmean", [P, 2], F32)
        h1 = sb("h1", [P, 2, BLK], F32)
        h2 = sb("h2", [P, BLK], F32)
        h3 = sb("h3", [P, BLK], F32)
        th = sb("th", [P, BLK], F32)
        cp = sb("cp", [P, BLK], F32)
        du = sb("du", [P, BLK], F32)
        dw = sb("dw", [P, BLK], F32)
        gv = sb("gv", [P, 4], F32)
        w1 = sb("w1", [P, 2, C], F32)
        w2 = sb("w2", [P, 2, P], F32)
        w3 = sb("w3", [P, P], F32)
        w4c = sb("w4c", [P, 1], F32)
        w4 = sb("w4", [P, P], F32)
        gw1 = sb("gw1", [P, 2, P], F32)
        gw2 = sb("gw2", [P, P], F32)
        gw3c = sb("gw3c", [P, 1], F32)
        gw3 = sb("gw3", [P, P], F32)
        bias = sb("bias", [P, 9], F32)
        halfb = sb("halfb", [P, 2], F32)
        sgn = sb("sgn", [P, 1], F32)
        cpl = sb("cpl", [P, 2], F32)

        PS = ctx.enter_context(nc.psum_tensor("PS", [P, 8, 512], F32))

        def bank(n):
            return PS[:, n, :]

        QB, KB, VB = PS[:, 0:2, :], PS[:, 2:4, :], PS[:, 4:6, :]
        TA, TB = 6, 7

        ld_ids, ld_small, ld_small2, ld_small3, ld_small4 = (sem(n) for n in ("ld_ids", "ld_small", "ld_small2", "ld_small3", "ld_small4"))
        ld_w = [sem(f"ld_w{i}") for i in range(6)]
        ld_u, ld_wp = sem("ld_u"), sem("ld_wp")
        idx_ready = sem("idx_ready")
        tok_in, spec_in = sem("tok_in"), sem("spec_in")
        small_in = [sem("small_in0"), sem("small_in1")]
        consts = sem("consts")
        wh_ready, w_split = sem("wh_ready"), sem("w_split")
        u_sq, u_norm = sem("u_sq"), sem("u_norm")
        dv, pl, ac = sem("dve_chain"), sem("pool_chain"), sem("act_chain")
        bn_ready, ln_sqrt, xn_ready, xt_done = sem("bn_ready"), sem("ln_sqrt"), sem("xn_ready"), sem("xt_done")
        xh_ready, xl_ready = sem("xh_ready"), sem("xl_ready")
        q_done, k_done, v_done, g_done = sem("q_done"), sem("k_done"), sem("v_done"), sem("g_done")
        sqq_ready, sqk_ready, redq_done, redk_done, sr_ready = (sem(n) for n in ("sqq_ready", "sqk_ready", "redq_done", "redk_done", "sr_ready"))
        qn_ready, kn_ready, kw_ready = sem("qn_ready"), sem("kn_ready"), sem("kw_ready")
        q_high, q_low, k_high, k_low = sem("q_high"), sem("q_low"), sem("k_high"), sem("k_low")
        trq_done, trk_done, stq_filled, stk_filled = sem("trq_done"), sem("trk_done"), sem("stq_filled"), sem("stk_filled")
        v_copied, gl_ready = sem("v_copied"), sem("gl_ready")
        v_stored = [sem("v_stored0"), sem("v_stored1")]
        q_stored, k_stored, c_stored = sem("q_stored"), sem("k_stored"), sem("c_stored")
        sp_neg, sp_exp, sp_ln, cp_ready, ct_done, ct_copied, bt_ready = (sem(n) for n in ("sp_neg", "sp_exp", "sp_ln", "cp_ready", "ct_done", "ct_copied", "bt_ready"))

        rows_set = sem("rows_set")
        ld_a1 = [sem("ld_a1_0"), sem("ld_a1_1")]
        ld_bm = [sem(f"ld_bm_{c}") for c in range(NB)]
        ld_a2 = [sem(f"ld_a2_{c}") for c in range(NB)]
        ld_b = [sem(f"ld_b_{c}") for c in range(NB)]
        ld_v = [sem(f"ld_v_{c}") for c in range(NB)]
        s_done, exp_done, pv_done = sem("s_done"), sem("exp_done"), sem("pv_done")
        sums = [sem("sums_a"), sem("sums_b")]
        mx_done, mx_read = sem("mx_done"), sem("mx_read")
        nm_ready, mrow_in = sem("nm_ready"), sem("mrow_in")
        misc_done, misc_read = sem("misc_done"), sem("misc_read")
        r_ready, o_done = sem("r_ready"), sem("o_done")

        ffz, ld_ff, ff_set = sem("ffz"), sem("ld_ff"), sem("ff_set")
        proj_done, h_added, bn2_ready, ln2_sqrt = sem("proj_done"), sem("h_added"), sem("bn2_ready"), sem("ln2_sqrt")
        x2_ready, x2t_done, tt_copied = sem("x2_ready"), sem("x2t_done"), sem("tt_copied")
        gmean_ready, g_mm, g_act, cpl_ready = sem("gmean_ready"), sem("g_mm"), sem("g_act"), sem("cpl_ready")
        l_done = [sem(f"l{i}_done") for i in range(1, 5)]
        a_done = [sem(f"a{i}_done") for i in range(1, 5)]
        dw_ready, t0_new, t1_new = sem("dw_ready"), sem("t0_new"), sem("t1_new")
        out_t, out_sum, out_stored = sem("out_t"), sem("out_sum"), sem("out_stored")
        att_over, ff_dve, cp_made, du_ready = sem("att_over"), sem("ff_dve"), sem("cp_made"), sem("du_ready")

        class Chain:

            def __init__(self, s):
                self.s, self.base, self.n = s, 0, 0

            def inc(self, ins):
                ins.then_inc(self.s, 1)
                self.n += 1

            def wait(self, eng):
                eng.wait_ge(self.s, self.base + self.n)

        def tiles(eng, step, per_chain=None, chain=None):
            for t in range(2):
                step(t, t, 0)
            if chain is not None:
                base = chain.base + chain.n
                start = chain.n
                chain.n = 0
            with eng.Fori(1, NT // 2 - 1) as n:
                if chain is not None:
                    chain.base = (n - 1) * (2 * per_chain) + base
                step(n * 2, 0, n)
                step(n * 2 + 1, 1, n)
            if chain is not None:
                assert chain.n == 2 * per_chain, chain.n
                chain.base, chain.n = base + (NT - 4) * per_chain, 0
            for t in range(NT - 2, NT):
                step(t, t % 2, t // 2)

        def s_bank(unit):
            return bank(unit % S_RING)

        def mx_bank(m):
            return bank(3 + m % MX_RING)

        def o_bank(b):
            return bank(5 + b % 2)

        MISC = 7
        PER_BODY = 2 * NSTEP
        T_AT = {4: (2,), 20: (3,), 32: (0, 1)}
        BLOCK_END = [BIAS_AT[b] + block_tiles(b) for b in range(NB)]
        MISC_USES = []
        for k in range(PER_BODY):
            par, s_ = divmod(k, NSTEP)
            for b in range(NB):
                if (BLOCK_END[b] + 3) == s_:
                    MISC_USES.append((k, "sums", par, b))
            if s_ == 3 and par == 1:
                MISC_USES.append((k, "sums", 0, NB - 1))
            if s_ - 1 in T_AT:
                MISC_USES.append((k, "row", par, T_AT[s_ - 1]))
        MISC_USES.append((PER_BODY, "sums", 1, NB - 1))
        NMISC = len(MISC_USES)

        def misc_at(k):
            return [(i, *use[1:]) for i, use in enumerate(MISC_USES) if use[0] == k]

        def row_index(par, blocks):
            return next(i for i, use in enumerate(MISC_USES) if use[1:] == ("row", par, blocks))

        def sums_index(par, b):
            return next(i for i, use in enumerate(MISC_USES) if use[1:] == ("sums", par, b))

        def max_units(k):
            par, s_ = divmod(k, NSTEP)
            for j in range(2):
                m = LEAD + 2 * s_ + j
                yield NMAX * par + m, (par + m // NMAX) % 2, m % NMAX

        BLOCK_STARTS = [0] + MAX_END[:-1]

        def max_shape(m):
            b, qt, hd, c = MAXES[m]
            return b, qt, hd, c, (P * (qt + 1) if c == b else BLK)

        block = ctx.enter_context(nc.Block())

        def add_up(e, eng, iv, k, hd):
            par, s_ = divmod(k, NSTEP)
            b, j = STEPS[s_]
            c0 = P * max(j - TPB * b, 0)
            done = iv * PER_BODY + k
            src = PB[:, (2 * k + hd) % P_RING, c0:]
            dst = acc[:, b % 2, hd, c0:]
            e.wait_ge(exp_done, done * 2 + hd + 1)
            if j == 0:
                if (par, b) not in ((0, 0), (0, 1)):
                    two_ago = (par, b - 2) if b >= 2 else (par - 1, b + 2)
                    e.wait_ge(misc_done, iv * NMISC + sums_index(*two_ago) + 2)
                eng.tensor_tensor(dst, src, ones[:, 0:1].broadcast_to([P, BLK]), ALU.mult).then_inc(sums[hd], 1)
            else:
                e.wait_ge(sums[hd], done)
                eng.tensor_tensor(dst, dst, src, ALU.add).then_inc(sums[hd], 1)

        @block.sync
        def _(sp_):
            e = sp_
            e.dma_start(ids[:, :], x.rearrange("o (t p) -> p (o t)", p=P), allow_slow_non_contiguous=True).then_inc(ld_ids, 16)
            for i, (tab, s) in enumerate(((op_table, ld_small), (var_table, ld_small2), (const_table, ld_small3), (struct_table, ld_small4))):
                e.dma_start(small_d[SMALL * i:SMALL * (i + 1), :], tab).then_inc(s, 16)
            e.dma_start(ub[:, :, :].rearrange("p h d -> p (h d)"),
                        u.rearrange("h d -> (h d)").rearrange("(o n) -> o n", o=1).broadcast_to([P, H * D])).then_inc(ld_u, 16)
            for dst, src in ((qwb, q_w), (kwb, k_w), (GL[:, NT, :], omega)):
                n = src.shape[0]
                dst = dst[:, :] if dst is qwb or dst is kwb else dst
                e.dma_start(dst, src.rearrange("(o n) -> o n", o=1).broadcast_to([P, n])).then_inc(ld_u, 16)
            n = 0
            for m, w in enumerate((wq, wk, wv)):
                for half in range(2):
                    if n >= 2:
                        e.wait_ge(w_split, n - 1)
                    e.dma_start(wst[:, n % 2, :], w[P * half:P * (half + 1), :]).then_inc(ld_w[n], 16)
                    n += 1
            e.dma_start(wp[:, :, :], wproj.rearrange("(a p) n -> p a n", p=P)).then_inc(ld_wp, 16)

            def store(t, r, n):
                at_least(e, v_copied, t + 1)
                e.dma_start(v_d[bass.ds(t * P, P), :], VS[:, r, :]).then_inc(v_stored[r], 16)
                if r == 0 and not (isinstance(t, int) and t == 0):
                    stage(n - 1)

            def stage(n):
                e.wait_ge(stq_filled, n * 4 + 4)
                e.dma_start(qT_d[:, :, bass.ds(n * (2 * P), 2 * P)].rearrange("h r t -> r h t"), STQ[:, :, :]).then_inc(q_stored, 16)
                e.wait_ge(stk_filled, n * 4 + 4)
                e.dma_start(kT_d[:, :, bass.ds(n * (2 * P), 2 * P)].rearrange("h r t -> r h t"), STK[:, :, :]).then_inc(k_stored, 16)

            tiles(e, store)
            stage(NT // 2 - 1)
            e.wait_ge(ct_copied, 2)
            e.dma_start(c_d, CT[:, :]).then_inc(c_stored, 16)
            e.wait_ge(c_stored, 16)
            for r in range(2):
                e.wait_ge(v_stored[r], 16 * (NT // 2))
            e.wait_ge(q_stored, 16 * (NT // 2))
            e.wait_ge(k_stored, 16 * (NT // 2))
            e.wait_ge(bt_ready, NB)
            e.wait_ge(rows_set, 7)

            def chunk(c):
                return slice(BLK * c, BLK * (c + 1))

            def load_a1(q, r):
                e.dma_start(A1[0:D, r, :, :], kT_d[bass.ds(q * 2, 2), 0:D, :].rearrange("h r t -> r h t")).then_inc(ld_a1[r], 16)
                e.dma_start(A1[D:D + NC, r, :, :], c_d.rearrange("(h k) t -> k h t", k=NC)[:, bass.ds(q * 2, 2), :]).then_inc(ld_a1[r], 16)

            def high_queries(dst, q, c, s):
                e.dma_start(dst[0:D, :, chunk(c)], qT_d[bass.ds(q * 2, 2), D:P, chunk(c)].rearrange("h r t -> r h t")).then_inc(s, 16)

            def load_b(q, c):
                high_queries(B1, q, c, ld_b[c])
                e.dma_start(B2[:, :, chunk(c)], qT_d[bass.ds(q * 2, 2), :, chunk(c)].rearrange("h r t -> r h t")).then_inc(ld_b[c], 16)

            def load_kv(q, c):
                e.dma_start(A2[:, :, chunk(c)], kT_d[bass.ds(q * 2, 2), :, chunk(c)].rearrange("h r t -> r h t")).then_inc(ld_a2[c], 16)
                e.dma_start(V[:, TPB * c:TPB * (c + 1), :],
                            v_d[chunk(c), bass.ds(q * P, P)].rearrange("(j p) n -> p j n", p=P)).then_inc(ld_v[c], 16)

            def load_rows(blocks, count):
                e.wait_ge(misc_read, count)
                for i, b in enumerate(blocks):
                    for hd in range(2):
                        at = 2 * TPB * i + TPB * hd
                        e.dma_start(B1[MAX_ROW:MAX_ROW + 1, hd, chunk(b)], mrow[at:at + TPB, :]).then_inc(mrow_in, 16)

            load_a1(0, 0)
            for c in range(NB):
                high_queries(BM, 0, c, ld_bm[c])
            for c in range(NB):
                load_b(0, c)
                load_kv(0, c)
            load_rows((0, 1), 1)
            with e.Fori(0, NP // 2) as iv:
                for par in range(2):
                    q = iv * 2 + par
                    nxt = iv * 2 + 1 if par == 0 else (iv * 2 + 2) % NP
                    e.wait_ge(pv_done, q * NSTEP + 1)
                    load_a1(nxt, 1 - par)
                    for c in (0, 1):
                        high_queries(BM, nxt, c, ld_bm[c])
                    for b in range(NB - 1):
                        e.wait_ge(s_done, q * (2 * NSTEP) + 2 * BLOCK_END[b])
                        load_b(nxt, b)
                        if b == 0:
                            load_rows((2,), iv * NMISC + row_index(par, (2,)) + 2)
                            e.wait_ge(mx_done, q * NMAX + MAX_END[2])
                            high_queries(BM, nxt, 2, ld_bm[2])
                        if b == 1:
                            load_rows((3,), iv * NMISC + row_index(par, (3,)) + 2)
                            e.wait_ge(mx_done, q * NMAX + MAX_END[3])
                            high_queries(BM, nxt, 3, ld_bm[3])
                    for c in range(NB):
                        e.wait_ge(pv_done, q * NSTEP + BIAS_AT[NB - 1] + TPB * (c + 1))
                        load_kv(nxt, c)
                        if c == 1:
                            load_rows((0, 1), iv * NMISC + row_index(par, (0, 1)) + 2)
                    load_b(nxt, NB - 1)
            for r in range(2):
                e.wait_ge(ld_a1[r], 32 * (NP // 2 + 1 - r))
            for c in range(NB):
                for s in (ld_a2[c], ld_bm[c], ld_v[c]):
                    e.wait_ge(s, 16 * (NP + 1))
                e.wait_ge(ld_b[c], 32 * (NP + 1))
            e.wait_ge(mrow_in, 64 + 128 * NP)
            e.wait_ge(o_done, 2 + NB * NP)
            e.nop().then_inc(att_over, 1)
            e.wait_ge(ffz, 5)
            loads = [(w1[:, :, :], cn_w1.rearrange("(a p) n -> p a n", p=P)), (w2[:, :, :], cn_w2.rearrange("(a p) n -> p a n", p=P)),
                     (w3[:, 0:D], cn_w3), (w4c[0:D, :], cn_w4), (gw1[:, :, :], gc_w1.rearrange("(a p) n -> p a n", p=P)),
                     (gw2[:, 0:D], gc_w2), (gw3c[0:D, :], gc_w3)]
            for i, (b_, n) in enumerate(((cn_b1[0:P], P), (cn_b1[P:C], P), (cn_b2, P), (cn_b3, D), (cn_b4, 0), (gc_b1, P), (gc_b2, D), (gc_b3, 0), (ada, 0))):
                src = b_.rearrange("(p o) -> p o", o=1) if n else b_.rearrange("(o n) -> o n", o=1).broadcast_to([P, 1])
                loads.append((bias[0:(n or P), i:i + 1], src))
            assert len(loads) == FF_LOADS
            for dst, src in loads:
                e.dma_start(dst, src).then_inc(ld_ff, 16)
            for b in range(NB):
                e.wait_ge(out_sum, 2 * (b + 1))
                e.dma_start(out[BLK * b:BLK * (b + 1), :].rearrange("(t p) c -> p t c", p=P), E[:, TPB * b:TPB * (b + 1), :]).then_inc(out_stored, 16)
            e.wait_ge(out_stored, 16 * NB)

        @block.gpsimd
        def _(e):
            g = nc.gpsimd
            ch = Chain(pl)
            e.wait_ge(ld_ids, 16)
            e.wait_ge(idx_ready, 1)
            for s in (ld_small, ld_small2, ld_small3, ld_small4):
                e.wait_ge(s, 16)

            def idx(a, t):
                return bass.IndirectOffsetOnAxis(ap=a[:, t:t + 1].bitcast(U32), axis=0)

            def gather(t):
                e.indirect_dma_start(E[:, t, 0:HALF], None, tok_table, idx(ids, t)).then_inc(tok_in, 16)
                e.indirect_dma_start(E[:, t, HALF:C], None, special_table, idx(spec_ids, t),
                                     bounds_check=special_table.shape[0] - 1, oob_is_err=False).then_inc(spec_in, 16)

            def gather_small(t):
                e.wait_ge(tok_in, 16 * (t + 1))
                e.wait_ge(spec_in, 16 * (t + 1))
                e.indirect_dma_start(E[:, t, HALF:C], None, small_d, idx(ids, t),
                                     bounds_check=NSMALL - 1, oob_is_err=False).then_inc(small_in[t % 2], 16)

            gather(0)
            gather_small(0)
            gather(1)
            gather_small(1)
            ch.inc(g.memset(ident[:, :], 1.0))
            ch.wait(e)
            ch.inc(g.affine_select(out=ident[:, :], in_=ident[:, :], compare_op=ALU.is_equal, fill=0.0,
                                   base=0, pattern=[[-1, P]], channel_multiplier=1))
            ch.wait(e)
            g.memset(eps_t[:, :], EPS).then_inc(consts, 1)
            g.tensor_copy(ident16[:, :], ident[:, :]).then_inc(consts, 1)
            g.tensor_copy(identb[:, :], ident[:, :]).then_inc(consts, 1)
            for t in (2, 3):
                gather(t)
                e.wait_ge(small_in[t % 2], 16)
                gather_small(t)
            ch.inc(g.memset(mask_s[:, :], 0.0))
            ch.inc(g.memset(mask_m[:, :], 0.0))
            ch.wait(e)
            g.affine_select(out=mask_s[:, :], in_=mask_s[:, :], compare_op=ALU.is_ge, fill=NEG,
                            base=0, pattern=[[1, P]], channel_multiplier=-1).then_inc(consts, 1)
            g.affine_select(out=mask_m[:, :], in_=mask_m[:, :], compare_op=ALU.is_ge, fill=NEG,
                            base=0, pattern=[[-1, P]], channel_multiplier=1).then_inc(consts, 1)
            for h in range(H):
                g.memset(slope[:, h:h + 1], 2.0 ** (-0.5 * (h + 1))).then_inc(consts, 1)
            for b in range(NB):
                n = block_tiles(b)
                g.iota(off_i[:, BIAS_AT[b]:BIAS_AT[b] + n], pattern=[[P, n]], base=-BLK * b, channel_multiplier=1).then_inc(consts, 1)
            for t in range(NT):
                r = t % 2
                if t + 4 < NT:
                    gather(t + 4)
                e.wait_ge(kn_ready, t + 1)
                at_least(e, k_low, t)
                g.tensor_tensor(KW[:, :, :], KN[:, :, :],
                                wqk[:, :].rearrange("p (o d) -> p o d", o=1).broadcast_to([P, H, D]), ALU.mult).then_inc(kw_ready, 1)
                if t + 4 < NT:
                    gather_small(t + 4)
                e.wait_ge(k_high, t + 1)
                g.tensor_tensor(KT[:, r, :, D:P], KW[:, :, :], KT[:, r, :, 0:D], ALU.subtract).then_inc(k_low, 1)
                if t >= 10:
                    e.wait_ge(k_low, t + 1)
                if t == 10:
                    g.memset(A1[96:P, :, :, :], 8.0).then_inc(rows_set, 1)
                    e.wait_ge(rows_set, 1)
                if t == 11:
                    g.memset(A1[D:MAX_ROW, :, :, :], 0.0).then_inc(rows_set, 1)
                    e.wait_ge(rows_set, 2)
                if t == 12:
                    g.memset(B1[D:P, :, :], 0.0).then_inc(rows_set, 1)
                    e.wait_ge(rows_set, 3)
                if t == 13:
                    g.memset(BM[D:P, :, :], 0.0).then_inc(rows_set, 1)
                    e.wait_ge(rows_set, 4)
                if t == 14:
                    g.iota(B1[D:D + 3, :, :], pattern=[[0, 2 * NB], [1, BLK]], base=0, channel_multiplier=0,
                           allow_small_or_imprecise_dtypes=True).then_inc(rows_set, 1)
                    g.memset(BM[D:D + NC, :, :], 64.0).then_inc(rows_set, 1)
                    e.wait_ge(rows_set, 6)
                if t == 15:
                    g.iota(BM[D:D + 3, :, :], pattern=[[0, 2], [1, T]], base=0, channel_multiplier=0,
                           allow_small_or_imprecise_dtypes=True).then_inc(rows_set, 1)
                    e.wait_ge(rows_set, 7)
            e.wait_ge(o_done, 2)
            with e.Fori(0, NP // 2) as iv:
                for k in range(PER_BODY):
                    add_up(e, g, iv, k, 1)
            e.wait_ge(att_over, 1)
            for z in (w3, w4, gw2, gw3, bias):
                g.memset(z[:, :], 0.0).then_inc(ffz, 1)
            g.memset(sgn[:, :], 1.0).then_inc(ffz, 1)
            e.wait_ge(ffz, 6)
            g.memset(sgn[D:P, :], -1.0).then_inc(ffz, 1)

            def update(n, b):
                e.wait_ge(dw_ready, n + 1)
                sl = slice(BLK * b, BLK * (b + 1))
                g.tensor_tensor(TT[:, 1, sl], TT[:, 1, sl], dw[:, :], ALU.subtract).then_inc(t1_new, 1)

            with e.Fori(0, CYCLES) as cyc:
                for b in range(NB):
                    update(cyc * NB + b, b)

        NCONST = 3 + 2 + H + NB

        @block.scalar
        def _(e):
            a = nc.scalar
            for n in range(6):
                e.wait_ge(ld_w[n], 16)
                a.activation(wh[:, n % 2, n // 2, :], wst[:, n % 2, :], ACT.Copy).then_inc(wh_ready, 1)
                if n == 1:
                    e.wait_ge(consts, 3)
                    for t in range(2):
                        e.wait_ge(bn_ready, t + 1)
                        a.activation(ls[:, t, :], mv[:, t, 1:2], ACT.Sqrt, bias=eps_t[:, 0:1]).then_inc(ln_sqrt, 1)
                    e.wait_ge(u_sq, 1)
                    a.activation(un[:, :], un[:, :], ACT.Sqrt).then_inc(u_norm, 1)
            e.wait_ge(xt_done, 1)
            a.activation(XH[:, 0, :, :].rearrange("p a n -> p (a n)"), bank(TA)[:, C:2 * C], ACT.Copy).then_inc(xh_ready, 1)

            def evac_q(t, r, n, k):
                e.wait_ge(trq_done, t * 2 + k + 1)
                if k == 0 and r == 0:
                    at_least(e, q_stored, n * 16)
                a.activation(STQ[:, 8 * k:8 * k + 8, P * r:P * (r + 1)],
                             bank((TB, TA)[k]).bitcast(F16).rearrange("p (h n) -> p h n", n=P), ACT.Copy).then_inc(stq_filled, 1)

            def keys_high(t, r):
                e.wait_ge(kw_ready, t + 1)
                a.activation(KT[:, r, :, 0:D], KW[:, :, :], ACT.Copy).then_inc(k_high, 1)

            def step(t, r, n):
                first, last = isinstance(t, int) and t == 0, isinstance(t, int) and t == NT - 1
                near_end = isinstance(t, int) and t >= NT - 2
                n_before = n - 1 if r == 0 else n
                if not first:
                    keys_high(t - 1, 1 - r)
                e.wait_ge(q_done, t + 1)
                at_least(e, redq_done, t)
                a.activation(SQ[:, 0:H, :].rearrange("p h d -> p (h d)"), QB.rearrange("p a n -> p (a n)"), ACT.Square).then_inc(sqq_ready, 1)
                e.wait_ge(k_done, t + 1)
                at_least(e, redk_done, t)
                a.activation(SQ[:, H:, :].rearrange("p h d -> p (h d)"), KB.rearrange("p a n -> p (a n)"), ACT.Square).then_inc(sqk_ready, 1)
                if not last:
                    e.wait_ge(xt_done, t + 2)
                    a.activation(XH[:, 1 - r, :, :].rearrange("p a n -> p (a n)"), bank(TA)[:, C:2 * C], ACT.Copy).then_inc(xh_ready, 1)
                e.wait_ge(redk_done, t + 1)
                a.activation(sr[:, :], ms[:, :], ACT.Sqrt, bias=eps_t[:, 0:1], scale=1.0 / D).then_inc(sr_ready, 1)
                if not first:
                    evac_q(t - 1, 1 - r, n_before, 0)
                if not near_end:
                    e.wait_ge(bn_ready, t + 3)
                    a.activation(ls[:, r, :], mv[:, r, 1:2], ACT.Sqrt, bias=eps_t[:, 0:1]).then_inc(ln_sqrt, 1)
                if not first:
                    evac_q(t - 1, 1 - r, n_before, 1)
                e.wait_ge(qn_ready, t + 1)
                a.activation(QT[:, r, :, D:P], QN[:, :, :], ACT.Copy).then_inc(q_high, 1)
                e.wait_ge(v_done, t + 1)
                at_least(e, v_stored[r], n * 16)
                a.activation(VS[:, r, :], VB.rearrange("p a n -> p (a n)"), ACT.Copy).then_inc(v_copied, 1)

            tiles(e, step)
            keys_high(NT - 1, 1)
            evac_q(NT - 1, 1, NT // 2 - 1, 0)
            evac_q(NT - 1, 1, NT // 2 - 1, 1)
            a.preload_act_table_set(EXP_LN_SET)
            e.wait_ge(sp_neg, 1)
            a.activation(na[:, :, :], na[:, :, :], ACT.Exp).then_inc(sp_exp, 1)
            e.wait_ge(sp_exp, 1)
            a.activation(na[:, :, :], na[:, :, :], ACT.Ln, bias=1.0).then_inc(sp_ln, 1)
            for k, tb in enumerate((TA, TB)):
                e.wait_ge(ct_done, k + 1)
                a.activation(CT[:, 1024 * k:1024 * (k + 1)], bank(tb)[0:NC * H, :].bitcast(F16), ACT.Copy).then_inc(ct_copied, 1)

            def row(n, count):
                e.wait_ge(misc_done, count)
                a.activation(mrow[0:n, :], bank(MISC)[0:n, 0:P // 2].bitcast(F16), ACT.Copy).then_inc(misc_read, 1)

            e.wait_ge(bt_ready, NB)
            row(2 * 2 * TPB, 1)
            with e.Fori(0, NP // 2) as iv:
                for k in range(PER_BODY):
                    par, s_ = divmod(k, NSTEP)
                    b, j = STEPS[s_]
                    c0 = P * max(j - TPB * b, 0)
                    q = iv * 2 + par
                    if s_ == 0:
                        a.activation(bts[:, par, :, :], BT[:, bass.ds(q * 2, 2), :], ACT.Copy).then_inc(ac, 1)
                        e.wait_ge(ac, q + 1)
                    for hd in range(2):
                        unit = 2 * k + hd
                        e.wait_ge(s_done, iv * (2 * PER_BODY) + unit + 1)
                        if unit >= P_RING:
                            e.wait_ge(pv_done, iv * PER_BODY + (unit - P_RING) // 2 + 1)
                            e.wait_ge(sums[hd], iv * PER_BODY + (unit - P_RING) // 2 + 1)
                        a.activation(PB[:, unit % P_RING, c0:], s_bank(unit)[:, c0:], ACT.Exp,
                                     bias=bts[:, par, hd, s_:s_ + 1], scale=0.125).then_inc(exp_done, 1)
                    for i, kind, upar, what in misc_at(k) + (misc_at(PER_BODY) if k == PER_BODY - 1 else []):
                        if kind == "row":
                            before = {(2,): 64, (3,): 96, (0, 1): 128}[what]
                            e.wait_ge(mrow_in, iv * 256 + 128 * upar + before)
                            row(2 * TPB * len(what), iv * NMISC + i + 2)
                        else:
                            e.wait_ge(misc_done, iv * NMISC + i + 2)
                            a.activation(lnr[:, :], bank(MISC), ACT.Ln).then_inc(misc_read, 1)
                            e.wait_ge(misc_read, iv * NMISC + i + 2)
                            e.wait_ge(o_done, iv * (2 * NB) + NB * upar + what + 2)
                            a.activation(R[:, :], lnr[:, :], ACT.Exp, scale=-1.0).then_inc(r_ready, 1)
            def transposed(t):
                for half in range(2):
                    e.wait_ge(x2t_done, t + 1)
                    a.activation(TT[:, half, P * t:P * (t + 1)], bank(2 + t % 2)[:, P * half:P * (half + 1)], ACT.Copy,
                                 accum_out=gm[:, half, t:t + 1]).then_inc(tt_copied, 1)

            for t in range(NT):
                e.wait_ge(bn2_ready, t + 1)
                a.activation(lsb[:, t % 2, :], mvb[:, t % 2, 1:2], ACT.Sqrt, bias=eps_t[:, 0:1]).then_inc(ln2_sqrt, 1)
                if t >= 2:
                    transposed(t - 2)
            transposed(NT - 2)
            transposed(NT - 1)
            e.wait_ge(ff_set, 4)
            for i, (f, b_, s) in enumerate(((ACT.Gelu, bias[:, 5:6], 1.0), (ACT.Gelu, bias[:, 6:7], 1.0), (ACT.Tanh, halfb[:, 1:2], 0.5))):
                e.wait_ge(g_mm, i + 1)
                a.activation(gv[:, i:i + 1], bank(5)[:, 0:1], f, bias=b_, scale=s).then_inc(g_act, 1)

            def gelu1(n):
                for half in range(2):
                    e.wait_ge(l_done[0], n * 2 + half + 1)
                    at_least(e, l_done[1], n)
                    a.activation(h1[:, half, :], bank(half), ACT.Gelu, bias=bias[:, half:half + 1]).then_inc(a_done[0], 1)

            def gelu2(n):
                e.wait_ge(l_done[1], n + 1)
                at_least(e, l_done[2], n)
                a.activation(h2[:, :], bank(2), ACT.Gelu, bias=bias[:, 2:3]).then_inc(a_done[1], 1)

            def gelu3(n):
                e.wait_ge(l_done[2], n + 1)
                at_least(e, l_done[3], n)
                a.activation(h3[:, :], bank(3), ACT.Gelu, bias=bias[:, 3:4]).then_inc(a_done[2], 1)

            def tanh(n):
                e.wait_ge(l_done[3], n + 1)
                at_least(e, cp_made, n)
                a.activation(th[:, :], bank(4), ACT.Tanh, bias=halfb[:, 0:1], scale=0.5).then_inc(a_done[3], 1)

            for n in range(NB):
                for late, layer in ((3, tanh), (2, gelu3), (1, gelu2), (0, gelu1)):
                    if n >= late:
                        layer(n - late)
            with e.Fori(1, CYCLES) as cyc:
                for b in range(NB):
                    for late, layer in ((3, tanh), (2, gelu3), (1, gelu2), (0, gelu1)):
                        layer(cyc * NB + (b - late))
            for n in range(CYCLES * NB, CYCLES * NB + 3):
                for late, layer in ((3, tanh), (2, gelu3), (1, gelu2)):
                    if n - late < CYCLES * NB:
                        layer(n - late)

        @block.tensor
        def _(e):
            pe = nc.tensor

            def xt(t_plus, r):
                e.wait_ge(xn_ready, t_plus)
                for half in range(2):
                    last = pe.transpose(bank(TA)[:, C + P * half:C + P * (half + 1)], XN[:, r, P * half:P * (half + 1)], ident[:, :])
                last.then_inc(xt_done, 1)

            def project(dst, m, r, chunks):
                for ck in chunks:
                    k = 0
                    for half in range(2):
                        for xs, ws in ((XH, wh), (XH, wl), (XL, wh)):
                            last = pe.matmul(dst[:, ck, :], xs[:, r, half, :], ws[:, half, m, 512 * ck:512 * (ck + 1)],
                                             start=k == 0, stop=k == 5)
                            k += 1
                return last

            def transposes(src, r, k, done):
                for h in range(8):
                    last = pe.transpose(bank((TB, TA)[k]).bitcast(F16)[:, P * h:P * (h + 1)], src[:, r, 8 * k + h, :], ident16[:, :])
                last.then_inc(done, 1)

            def first_queries(t, r):
                e.wait_ge(q_high, t + 1)
                e.wait_ge(q_low, t + 1)
                transposes(QT, r, 0, trq_done)

            def keys(t, r):
                e.wait_ge(k_high, t + 1)
                e.wait_ge(k_low, t + 1)
                for k in range(2):
                    e.wait_ge(stq_filled, t * 2 + k + 1)
                    transposes(KT, r, k, trk_done)

            def step(t, r, n):
                first, last_t = isinstance(t, int) and t == 0, isinstance(t, int) and t == NT - 1
                e.wait_ge(xh_ready, t + 1)
                e.wait_ge(xl_ready, t + 1)
                at_least(e, qn_ready, t)
                project(QB, 0, r, (0, 1)).then_inc(q_done, 1)
                at_least(e, kn_ready, t)
                project(KB, 1, r, (0, 1)).then_inc(k_done, 1)
                at_least(e, stk_filled, t * 2 - 2)
                k = 0
                for half in range(2):
                    for xs, ws in ((XH, wgh), (XH, wgl), (XL, wgh)):
                        last = pe.matmul(bank(TA)[:, 0:H], xs[:, r, half, :], ws[:, half, :], start=k == 0, stop=k == 5)
                        k += 1
                last.then_inc(g_done, 1)
                if not last_t:
                    xt(t + 2, 1 - r)
                if not first:
                    first_queries(t - 1, 1 - r)
                at_least(e, v_copied, t)
                project(VB, 2, r, (0,))
                if not first:
                    e.wait_ge(gl_ready, t + 1)
                    if not last_t:
                        e.wait_ge(xl_ready, t + 2)
                    transposes(QT, 1 - r, 1, trq_done)
                project(VB, 2, r, (1,)).then_inc(v_done, 1)
                if not first:
                    keys(t - 1, 1 - r)

            e.wait_ge(consts, 3)
            xt(1, 0)
            e.wait_ge(w_split, 7)
            tiles(e, step)
            e.wait_ge(stk_filled, 2 * NT - 2)
            first_queries(NT - 1, 1)
            transposes(QT, 1, 1, trq_done)
            keys(NT - 1, 1)
            e.wait_ge(cp_ready, 2)
            for k, tb in enumerate((TA, TB)):
                e.wait_ge(stk_filled, 2 * NT)
                for t in range(8):
                    last = pe.transpose(bank(tb).bitcast(F16)[0:NC * H, P * t:P * (t + 1)],
                                        CP[:, 8 * k + t, :, :].rearrange("p h n -> p (h n)"), ident16[:, :])
                last.then_inc(ct_done, 1)

            def max_unit(m, r):
                b, qt, hd, c, n = max_shape(m)
                dst = mx_bank(m)[:, 0:n]
                q0 = BLK * b + P * qt
                last = pe.matmul(dst, BM[:, hd, q0:q0 + P], A1[:, r, hd, BLK * c:BLK * c + n], start=True, stop=c != b)
                if c == b:
                    last = pe.matmul(dst[:, P * qt:], identb[:, :], mask_m[:, :], start=False, stop=True)
                last.then_inc(mx_done, 1)

            def transpose_rows(n):
                pe.transpose(bank(MISC)[0:n, 0:P // 2].bitcast(F16), nm[:, 0:n // (2 * TPB), :, :].rearrange("p b h t -> p (b h t)"), ident16[:, :]).then_inc(misc_done, 1)

            e.wait_ge(consts, NCONST)
            e.wait_ge(ct_copied, 2)
            e.wait_ge(ld_a1[0], 32)
            for m in range(LEAD):
                if m in BLOCK_STARTS:
                    e.wait_ge(ld_bm[MAXES[m][0]], 16)
                at_least(e, mx_read, m - 1)
                max_unit(m, 0)
            e.wait_ge(nm_ready, 1)
            transpose_rows(2 * 2 * TPB)
            with e.Fori(0, NP // 2) as iv:
                def pv(k):
                    par, s_ = divmod(k, NSTEP)
                    b, j = STEPS[s_]
                    c0 = P * max(j - TPB * b, 0)
                    q = iv * 2 + par
                    if j == 0:
                        e.wait_ge(o_done, q * NB + b + 1)
                    if j >= TPB * b and j % TPB == 0:
                        e.wait_ge(ld_v[b], q * 16 + 16)
                    e.wait_ge(exp_done, iv * (2 * PER_BODY) + 2 * k + 2)
                    for hd in range(2):
                        rows = slice(D * hd, D * (hd + 1))
                        last = pe.matmul(o_bank(b)[rows, c0:], V[:, j, rows], PB[:, (2 * k + hd) % P_RING, c0:],
                                         start=j == 0, stop=j == block_tiles(b) - 1)
                    last.then_inc(pv_done, 1)

                def misc(k):
                    for i, kind, upar, what in misc_at(k):
                        e.wait_ge(misc_read, iv * NMISC + i + 1)
                        if kind == "row":
                            e.wait_ge(nm_ready, iv * 6 + 3 * upar + {(2,): 2, (3,): 3, (0, 1): 4}[what])
                            transpose_rows(2 * TPB * len(what))
                        else:
                            for hd in range(2):
                                e.wait_ge(sums[hd], iv * PER_BODY + NSTEP * upar + BLOCK_END[what])
                                last = pe.matmul(bank(MISC)[D * hd:D * (hd + 1), :], ones[:, :], acc[:, what % 2, hd, :], start=True, stop=True)
                            last.then_inc(misc_done, 1)

                for k in range(PER_BODY):
                    par, s_ = divmod(k, NSTEP)
                    b, j = STEPS[s_]
                    c0 = P * max(j - TPB * b, 0)
                    q = iv * 2 + par
                    if j == 0:
                        e.wait_ge(ld_b[b], q * 32 + 32)
                        e.wait_ge(mrow_in, q * 128 + {0: 64, 1: 64, 2: 96, 3: 128}[b])
                    if j >= TPB * b and j % TPB == 0:
                        e.wait_ge(ld_a2[b], q * 16 + 16)
                    units = list(max_units(k))
                    for hd in range(2):
                        unit = 2 * k + hd
                        if unit >= S_RING:
                            e.wait_ge(exp_done, iv * (2 * PER_BODY) + unit - S_RING + 1)
                        dst = s_bank(unit)[:, c0:]
                        keys, queries = slice(P * j, P * (j + 1)), slice(BLK * b + c0, BLK * (b + 1))
                        pe.matmul(dst, A1[:, par, hd, keys], B1[:, hd, queries], start=True, stop=False)
                        if j >= TPB * b:
                            pe.matmul(dst[:, 0:P], identb[:, :], mask_s[:, :], start=False, stop=False)
                        pe.matmul(dst, A2[:, hd, keys], B2[:, hd, queries], start=False, stop=True).then_inc(s_done, 1)
                        at, mpar, m = units[hd]
                        if m == 0:
                            e.wait_ge(ld_a1[mpar], iv * 32 + 32 * (2 if par else 1))
                        if m in BLOCK_STARTS:
                            e.wait_ge(ld_bm[MAXES[m][0]], iv * 32 + 16 * (at // NMAX) + 16)
                        e.wait_ge(mx_read, iv * (2 * NMAX) + at - 1)
                        max_unit(m, mpar)
                    if k >= 2:
                        pv(k - 2)
                    misc(k)
                pv(PER_BODY - 2)
                pv(PER_BODY - 1)
                misc(PER_BODY)
            def stream_transpose(t):
                e.wait_ge(x2_ready, t + 1)
                at_least(e, tt_copied, 2 * t - 2)
                for half in range(2):
                    last = pe.transpose(bank(2 + t % 2)[:, P * half:P * (half + 1)], X2[:, t % 2, P * half:P * (half + 1)], ident[:, :])
                last.then_inc(x2t_done, 1)

            e.wait_ge(ld_wp, 16)
            e.wait_ge(att_over, 1)
            for t in range(NT):
                at_least(e, h_added, t - 1)
                for pair in range(NP):
                    last = pe.matmul(bank(t % 2)[:, 0:C], OT[:, pair, P * t:P * (t + 1)], wp[:, pair, :], start=pair == 0, stop=pair == NP - 1)
                last.then_inc(proj_done, 1)
                if t >= 2:
                    stream_transpose(t - 2)
            stream_transpose(NT - 2)
            stream_transpose(NT - 1)
            e.wait_ge(ff_set, 4)
            e.wait_ge(gmean_ready, 1)
            for half in range(2):
                last = pe.matmul(bank(5)[:, 0:1], gw1[:, half, :], gmean[:, half:half + 1], start=half == 0, stop=half == 1)
            last.then_inc(g_mm, 1)
            for i, w in enumerate((gw2, gw3)):
                e.wait_ge(g_act, i + 1)
                pe.matmul(bank(5)[:, 0:1], w[:, :], gv[:, i:i + 1], start=True, stop=True).then_inc(g_mm, 1)

            def layer1(n, b):
                if not isinstance(n, int) or n >= NB:
                    e.wait_ge(t0_new, n - (NB - 1))
                    e.wait_ge(t1_new, n - (NB - 1))
                for out_half in range(2):
                    at_least(e, a_done[0], n * 2 - 1 + out_half)
                    for half in range(2):
                        last = pe.matmul(bank(out_half), w1[:, half, P * out_half:P * (out_half + 1)], TT[:, half, BLK * b:BLK * (b + 1)],
                                         start=half == 0, stop=half == 1)
                    last.then_inc(l_done[0], 1)

            def layer2(n, b):
                e.wait_ge(a_done[0], n * 2 + 2)
                at_least(e, a_done[1], n)
                for half in range(2):
                    last = pe.matmul(bank(2), w2[:, half, :], h1[:, half, :], start=half == 0, stop=half == 1)
                last.then_inc(l_done[1], 1)

            def layer3(n, b):
                e.wait_ge(a_done[1], n + 1)
                at_least(e, a_done[2], n)
                pe.matmul(bank(3), w3[:, :], h2[:, :], start=True, stop=True).then_inc(l_done[2], 1)

            def layer4(n, b):
                e.wait_ge(a_done[2], n + 1)
                at_least(e, a_done[3], n)
                pe.matmul(bank(4), w4[:, :], h3[:, :], start=True, stop=True).then_inc(l_done[3], 1)

            def stream_back(b):
                e.wait_ge(t0_new, (CYCLES - 1) * NB + b + 1)
                e.wait_ge(t1_new, (CYCLES - 1) * NB + b + 1)
                for pr in range(2 * b, 2 * b + 2):
                    at_least(e, out_sum, pr - 1)
                    for i in range(2):
                        t = 2 * pr + i
                        for half in range(2):
                            last = pe.transpose(bank(6 + pr % 2)[:, C * i + P * half:C * i + P * (half + 1)], TT[:, half, P * t:P * (t + 1)], ident[:, :])
                    last.then_inc(out_t, 1)

            e.wait_ge(tt_copied, 2 * NT)
            for n in range(NB):
                for late, layer in ((3, layer4), (2, layer3), (1, layer2), (0, layer1)):
                    if n >= late:
                        layer(n - late, n - late)
            with e.Fori(1, CYCLES) as cyc:
                for b in range(NB):
                    for late, layer in ((3, layer4), (2, layer3), (1, layer2), (0, layer1)):
                        layer(cyc * NB + (b - late), (b - late) % NB)
            for n in range(CYCLES * NB, CYCLES * NB + 3):
                for late, layer in ((3, layer4), (2, layer3), (1, layer2)):
                    if n - late < CYCLES * NB:
                        layer(n - late, (n - late) % NB)
                stream_back(n - CYCLES * NB)
            stream_back(NB - 1)

        @block.vector
        def _(e):
            v = nc.vector
            ch = Chain(dv)
            e.wait_ge(ld_ids, 16)
            ch.inc(v.tensor_scalar(far[:, :], ids[:, :], float(NSMALL), FAR, ALU.is_lt, ALU.mult))
            ch.wait(e)
            v.scalar_tensor_tensor(spec_ids[:, :], ids[:, :], -float(NSMALL), far[:, :], ALU.add, ALU.add).then_inc(idx_ready, 1)

            e.wait_ge(ld_u, 64)
            ch.inc(v.tensor_tensor(tmp[:, :, :], ub[:, :, :], ub[:, :, :], ALU.mult))
            ch.wait(e)
            v.tensor_reduce(un[:, :], tmp[:, :, :], AX.X, ALU.add).then_inc(u_sq, 1)
            v.tensor_tensor(wqk[:, :], qwb[:, :], kwb[:, :], ALU.mult)
            ch.inc(v.tensor_tensor(ub[:, :, :], ub[:, :, :], kwb[:, :].rearrange("p (o d) -> p o d", o=1).broadcast_to([P, H, D]), ALU.mult))

            def stats(t, r, n):
                e.wait_ge(tok_in, t * 16 + 16)
                e.wait_ge(spec_in, t * 16 + 16)
                e.wait_ge(small_in[r], n * 16 + 16)
                tile = E[:, bass.ds(t, 1), :].rearrange("p o c -> p (o c)")
                ch.inc(v.bn_stats(bn6[:, r, :], tile))

            def aggregate(r):
                v.bn_aggr(mv[:, r, :], bn6[:, r, :]).then_inc(bn_ready, 1)

            def norm(t, r):
                e.wait_ge(ln_sqrt, t + 1)
                ch.inc(v.reciprocal(lr[:, r, :], ls[:, r, :]))
                ch.wait(e)
                at_least(e, xt_done, t - 1)
                tile = E[:, bass.ds(t, 1), :].rearrange("p o c -> p (o c)")
                v.tensor_scalar(XN[:, r, :], tile, mv[:, r, 0:1], lr[:, r, 0:1], ALU.subtract, ALU.mult).then_inc(xn_ready, 1)

            def split_w(n):
                e.wait_ge(wh_ready, n + 1)
                v.tensor_tensor(wl[:, n % 2, n // 2, :], wst[:, n % 2, :], wh[:, n % 2, n // 2, :].bitcast(F32), ALU.subtract).then_inc(w_split, 1)

            split_w(0)
            split_w(1)
            for t in range(2):
                stats(t, t, 0)
                ch.wait(e)
                aggregate(t)
            norm(0, 0)
            norm(1, 1)
            e.wait_ge(u_norm, 1)
            ch.inc(v.tensor_scalar(un[:, :], un[:, :], U_EPS, float(D) ** 0.5, ALU.max, ALU.mult))
            ch.wait(e)
            ch.inc(v.reciprocal(un[:, :], un[:, :]))
            for half in range(2):
                e.wait_ge(ld_w[2 + half], 16)
                ch.wait(e)
                ch.inc(v.tensor_tensor(tmp[:, :, :], wst[:, half, :].rearrange("p (h d) -> p h d", d=D), ub[:, :, :], ALU.mult))
                ch.wait(e)
                ch.inc(v.tensor_reduce(wgf[:, half, :], tmp[:, :, :], AX.X, ALU.add))
                ch.wait(e)
                ch.inc(v.tensor_tensor(wgf[:, half, :], wgf[:, half, :], un[:, :], ALU.mult))
                split_w(2 + half)
            ch.wait(e)
            ch.inc(v.tensor_copy(wgh[:, :, :], wgf[:, :, :]))
            ch.wait(e)
            v.tensor_tensor(wgl[:, :, :], wgf[:, :, :], wgh[:, :, :].bitcast(F32), ALU.subtract).then_inc(w_split, 1)
            split_w(4)
            split_w(5)

            def xt_low(t_plus, r):
                e.wait_ge(xh_ready, t_plus)
                v.tensor_tensor(XL[:, r, :, :].rearrange("p a n -> p (a n)"), bank(TA)[:, C:2 * C],
                                XH[:, r, :, :].rearrange("p a n -> p (a n)").bitcast(F32), ALU.subtract).then_inc(xl_ready, 1)

            xt_low(1, 0)

            def evac_k(t, r, n):
                for k in range(2):
                    e.wait_ge(trk_done, t * 2 + k + 1)
                    if k == 0 and r == 0:
                        at_least(e, k_stored, n * 16)
                    v.tensor_copy(STK[:, 8 * k:8 * k + 8, P * r:P * (r + 1)],
                                  bank((TB, TA)[k]).bitcast(F16).rearrange("p (h n) -> p h n", n=P)).then_inc(stk_filled, 1)

            def step(t, r, n):
                first, last = isinstance(t, int) and t == 0, isinstance(t, int) and t == NT - 1
                near_end = isinstance(t, int) and t >= NT - 2
                e.wait_ge(sqq_ready, t + 1)
                v.tensor_reduce(ms[:, 0:H], SQ[:, 0:H, :], AX.X, ALU.add).then_inc(redq_done, 1)
                e.wait_ge(sqk_ready, t + 1)
                v.tensor_reduce(ms[:, H:], SQ[:, H:, :], AX.X, ALU.add).then_inc(redk_done, 1)
                if not last:
                    xt_low(t + 2, 1 - r)
                if not near_end:
                    stats(t + 2, r, n + 1)
                    ch.wait(e)
                e.wait_ge(sr_ready, t + 1)
                ch.inc(v.reciprocal(rr[:, :], sr[:, :]))
                if not near_end:
                    aggregate(r)
                ch.wait(e)
                e.wait_ge(g_done, t + 1)
                v.tensor_tensor(GL[:, bass.ds(t, 1), :].rearrange("p o h -> p (o h)"), bank(TA)[:, 0:H], rr[:, H:2 * H], ALU.mult).then_inc(gl_ready, 1)
                for dst, src, k, s in ((QN, QB, 0, qn_ready), (KN, KB, 1, kn_ready)):
                    if k == 1:
                        at_least(e, kw_ready, t)
                    v.tensor_tensor(dst[:, :, :], src.rearrange("p a (h d) -> p (a h) d", d=D),
                                    rr[:, H * k:H * (k + 1)].rearrange("p (h o) -> p h o", o=1).broadcast_to([P, H, D]), ALU.mult).then_inc(s, 1)
                if not near_end:
                    norm(t + 2, r)
                e.wait_ge(q_high, t + 1)
                v.tensor_tensor(QT[:, r, :, 0:D], QN[:, :, :], QT[:, r, :, D:P], ALU.subtract).then_inc(q_low, 1)
                if not first:
                    evac_k(t - 1, 1 - r, n - 1 if r == 0 else n)

            tiles(e, step, 3, ch)
            evac_k(NT - 1, 1, NT // 2 - 1)
            e.wait_ge(gl_ready, NT)
            ch.inc(v.tensor_scalar(na[:, :, :], GL[:, :, :], -1.0, None, ALU.mult))
            ch.wait(e)
            v.tensor_tensor(na[:, :, :], na[:, :, :], GL[:, :, :], ALU.min).then_inc(sp_neg, 1)
            ch.inc(v.tensor_scalar(sp[:, :, :], GL[:, :, :], 0.0, None, ALU.max))
            e.wait_ge(sp_ln, 1)
            ch.wait(e)
            ch.inc(v.tensor_tensor(sp[:, :, :], sp[:, :, :], na[:, :, :], ALU.add))
            ch.wait(e)
            e.wait_ge(consts, NCONST)
            ch.inc(v.tensor_tensor(cw[:, :], sp[:, NT, :], slope[:, :], ALU.mult))
            ch.inc(v.tensor_copy(off[:, :], off_i[:, :]))
            ch.wait(e)
            ch.inc(v.tensor_tensor(cc[:, :, :], sp[:, 0:NT, :], cw[:, :].rearrange("p (o h) -> p o h", o=1).broadcast_to([P, NT, H]), ALU.mult))
            ch.wait(e)
            ch.inc(v.tensor_scalar(rest[:, :, :], cc[:, :, :], -8.0, None, ALU.mult))
            ch.inc(v.tensor_scalar(at_j[:, :], off[:, BIAS_AT[NB - 1]:], float(BLK * (NB - 1)), 0.125, ALU.add, ALU.mult))
            ch.wait(e)
            ch.inc(v.tensor_tensor(jc[:, :, :], cc[:, :, :], at_j[:, :].rearrange("p (t o) -> p t o", o=1).broadcast_to([P, NT, H]), ALU.mult))
            for whole, k, end in ((rest, 0, False), (rest, 1, False), (rest, 2, True), (jc, 3, False), (jc, 4, True)):
                ch.wait(e)
                if end:
                    v.tensor_copy(CP[:, :, :, k], whole[:, :, :]).then_inc(cp_ready, 1)
                else:
                    ch.inc(v.tensor_copy(CP[:, :, :, k], whole[:, :, :]))
                    ch.wait(e)
                    ch.inc(v.tensor_tensor(whole[:, :, :], whole[:, :, :], CP[:, :, :, k], ALU.subtract))
            for b in range(NB):
                n, o = block_tiles(b), BIAS_AT[b]
                v.tensor_tensor(BT[:, :, o:o + n], cc[:, 0:n, :].rearrange("p t h -> p h t"),
                                off[:, o:o + n].rearrange("p (o n) -> p o n", o=1).broadcast_to([P, H, n]), ALU.mult).then_inc(bt_ready, 1)

            e.wait_ge(k_stored, 16 * (NT // 2))
            e.wait_ge(v_stored[1], 16 * (NT // 2))
            e.wait_ge(c_stored, 16)
            v.memset(ones[:, :], 1.0).then_inc(o_done, 2)

            def max_read(m, r, count):
                b, qt, hd, c, n = max_shape(m)
                e.wait_ge(mx_done, count)
                v.tensor_reduce(mxp[:, r, b, 2 * qt + hd, c:c + 1], mx_bank(m)[:, 0:n], AX.X, ALU.max).then_inc(mx_read, 1)

            def negate(r, blocks, reads, links):
                e.wait_ge(mx_read, reads)
                for i, b in enumerate(blocks):
                    v.tensor_reduce(nmf[:, i, :, :].rearrange("p t h -> p (t h)"), mxp[:, r, b, :, 0:b + 1], AX.X, ALU.max).then_inc(dv, 1)
                e.wait_ge(dv, links)
                for i in range(len(blocks)):
                    ins = v.tensor_scalar(nm[:, i, :, :].rearrange("p h t -> p t h"), nmf[:, i, :, :], -0.125, None, ALU.mult)
                ins.then_inc(nm_ready, 1)

            for m in range(LEAD):
                max_read(m, 0, m + 1)
            dv0 = ch.base + ch.n
            negate(0, (0, 1), LEAD, dv0 + 2)
            with e.Fori(0, NP // 2) as iv:
                def output(upar, b):
                    q = iv * 2 + upar
                    e.wait_ge(r_ready, q * NB + b + 1)
                    v.tensor_tensor(OT[:, bass.ds(q, 1), BLK * b:BLK * (b + 1)].rearrange("p o t -> p (o t)"), o_bank(b), R[:, :], ALU.mult).then_inc(o_done, 1)

                for k in range(PER_BODY):
                    par, s_ = divmod(k, NSTEP)
                    for at, mpar, m in max_units(k):
                        max_read(m, mpar, iv * (2 * NMAX) + at + 1)
                    if s_ in T_AT:
                        blocks = T_AT[s_]
                        r = 1 - par if blocks == (0, 1) else par
                        rows = [i for i, use in enumerate(MISC_USES) if use[1] == "row" and use[0] <= k]
                        e.wait_ge(misc_done, iv * NMISC + (rows[-1] + 2 if rows else 1))
                        negate(r, blocks, iv * (2 * NMAX) + at + 1, iv * 8 + dv0 + 2 + 4 * par + {4: 1, 20: 2, 32: 4}[s_])
                    if k >= 1:
                        add_up(e, v, iv, k - 1, 0)
                    for i, kind, upar, what in misc_at(k - 1):
                        if kind == "sums":
                            output(upar, what)
                add_up(e, v, iv, PER_BODY - 1, 0)
                output(1, NB - 1)
            fd = Chain(ff_dve)

            def norm2(t):
                e.wait_ge(ln2_sqrt, t + 1)
                fd.inc(v.reciprocal(lrb[:, t % 2, :], lsb[:, t % 2, :]))
                fd.wait(e)
                at_least(e, x2t_done, t - 1)
                v.tensor_scalar(X2[:, t % 2, :], E[:, t, :], mvb[:, t % 2, 0:1], lrb[:, t % 2, :], ALU.subtract, ALU.mult).then_inc(x2_ready, 1)

            for t in range(NT):
                e.wait_ge(proj_done, t + 1)
                v.tensor_tensor(E[:, t, :], bank(t % 2)[:, 0:C], E[:, t, :], ALU.add).then_inc(h_added, 1)
                e.wait_ge(h_added, t + 1)
                fd.inc(v.bn_stats(bn6b[:, t % 2, :], E[:, t, :]))
                fd.wait(e)
                v.bn_aggr(mvb[:, t % 2, :], bn6b[:, t % 2, :]).then_inc(bn2_ready, 1)
                if t >= 1:
                    norm2(t - 1)
            norm2(NT - 1)
            e.wait_ge(ld_ff, FF_LOADS * 16)
            e.wait_ge(ffz, 7)
            for dst, src in ((w4, w4c), (gw3, gw3c)):
                v.tensor_copy(dst[0:D, :], src[0:D, :].broadcast_to([D, P])).then_inc(ff_set, 1)
            v.tensor_scalar(halfb[:, 0:1], bias[:, 4:5], 0.5, None, ALU.mult).then_inc(ff_set, 1)
            v.tensor_scalar(halfb[:, 1:2], bias[:, 7:8], 0.5, None, ALU.mult).then_inc(ff_set, 1)
            e.wait_ge(tt_copied, 2 * NT)
            fd.inc(v.tensor_reduce(gmean[:, :], gm[:, :, :], AX.X, ALU.add))
            fd.wait(e)
            v.tensor_scalar(gmean[:, :], gmean[:, :], 1.0 / T, None, ALU.mult).then_inc(gmean_ready, 1)
            fd.inc(v.tensor_scalar(cpl[:, 0:1], bias[:, 8:9], sgn[:, 0:1], 0.3, ALU.mult, ALU.mult))
            e.wait_ge(g_act, 3)
            fd.inc(v.tensor_scalar(gv[:, 3:4], gv[:, 2:3], bias[:, 8:9], 0.7, ALU.mult, ALU.mult))
            fd.wait(e)
            fd.inc(v.tensor_scalar(cpl[:, 1:2], gv[:, 3:4], 0.1, sgn[:, 0:1], ALU.add, ALU.mult))
            fd.wait(e)

            def update(n, b):
                sl = slice(BLK * b, BLK * (b + 1))
                e.wait_ge(a_done[3], n + 1)
                at_least(e, dw_ready, n)
                v.tensor_scalar(cp[:, :], th[:, :], cpl[:, 0:1], cpl[:, 1:2], ALU.mult, ALU.add).then_inc(cp_made, 1)
                e.wait_ge(cp_made, n + 1)
                v.tensor_tensor(du[:, :], cp[:, :], TT[:, 1, sl], ALU.mult).then_inc(du_ready, 1)
                at_least(e, t1_new, n)
                v.tensor_tensor(dw[:, :], cp[:, :], TT[:, 0, sl], ALU.mult).then_inc(dw_ready, 1)
                e.wait_ge(du_ready, n + 1)
                v.tensor_tensor(TT[:, 0, sl], TT[:, 0, sl], du[:, :], ALU.add).then_inc(t0_new, 1)

            def add_back(b):
                for pr in range(2 * b, 2 * b + 2):
                    e.wait_ge(out_t, pr + 1)
                    v.tensor_tensor(E[:, 2 * pr:2 * pr + 2, :].rearrange("p t c -> p (t c)"), bank(6 + pr % 2),
                                    E[:, 2 * pr:2 * pr + 2, :].rearrange("p t c -> p (t c)"), ALU.add).then_inc(out_sum, 1)

            update(0, 0)
            with e.Fori(1, CYCLES) as cyc:
                for b in range(1 - NB, 1):
                    update(cyc * NB + b, b % NB)
            for b in range(1, NB):
                update((CYCLES - 1) * NB + b, b)
                add_back(b - 1)
            add_back(NB - 1)


_INS = ["x", "L0_tok_token_table", "L0_tok_op_table", "L0_tok_var_table", "L0_tok_const_table", "L0_tok_struct_table", "L0_tok_special_table",
        "L0_attn_Wq", "L0_attn_Wk", "L0_attn_Wv", "L0_attn_Wproj", "L0_attn_q_rms_w", "L0_attn_k_rms_w", "L0_attn_omega", "L0_attn_u",
        "L0_ffn_cn_w1", "L0_ffn_cn_b1", "L0_ffn_cn_w2", "L0_ffn_cn_b2", "L0_ffn_cn_w3", "L0_ffn_cn_b3", "L0_ffn_cn_w4", "L0_ffn_cn_b4",
        "L0_ffn_gc_w1", "L0_ffn_gc_b1", "L0_ffn_gc_w2", "L0_ffn_gc_b2", "L0_ffn_gc_w3", "L0_ffn_gc_b3", "L0_ffn_adaptive_range"]


def kernel(**inputs):
    import numpy as _np
    import concourse.bacc as _bacc
    from concourse import mybir as _mybir
    from concourse.bass_utils import run_bass_kernel_spmd as _run

    nc = _bacc.Bacc("TRN2", target_bir_lowering=False, num_devices=1)
    arrays, args = {}, []
    for name in _INS:
        a = _np.ascontiguousarray(inputs[name])
        arrays[f"in_{name}_dram"] = a
        args.append(nc.dram_tensor(f"in_{name}_dram", a.shape, _mybir.dt.from_np(a.dtype), kind="ExternalInput").ap())
    args.append(nc.dram_tensor("out_0_dram", (T, C), F32, kind="ExternalOutput").ap())
    tower(nc, *args)
    r = _run(nc, [arrays], core_ids=[0])
    return r.results[0]["out_0_dram"].reshape(1, T, C)
```

```python
import concourse.bass as bass
from concourse import mybir
from contextlib import ExitStack

F32 = mybir.dt.float32
F32R = mybir.dt.float32r
F16 = mybir.dt.float16
BF16 = mybir.dt.bfloat16
I32 = mybir.dt.int32
U32 = mybir.dt.uint32
ALU = mybir.AluOpType
ACT = mybir.ActivationFunctionType
AX = mybir.AxisListType

T = 2048
HALF = 128
C = 256
H = 16
D = 64
P = 128
NT = T // P
NP = H // 2
BLK = 512
NB = T // BLK
TPB = BLK // P
SMALL = 10
NSMALL = 4 * SMALL
CYCLES = 3
FF_LOADS = 16
EXP_LN_SET = "natural_log_exp_and_others"
EPS = 1e-5
U_EPS = 1e-6
NEG = -1e30
FAR = 1e6
NC = 5
MAX_ROW = P - 1
S_RING, MX_RING, P_RING = 3, 2, 10
WST = 4


def at_least(eng, sem, value):
    if isinstance(value, int) and value <= 0:
        return
    eng.wait_ge(sem, value)


def block_tiles(b):
    return TPB * (b + 1)


BIAS_AT = [sum(block_tiles(x) for x in range(b)) for b in range(NB)]
STEPS = [(b, j) for b in range(NB) for j in range(block_tiles(b))]
NSTEP = len(STEPS)
MAXES = [(b, q, hd, ch) for b in range(NB) for q in range(TPB) for hd in range(2) for ch in range(b + 1)]
NMAX = len(MAXES)
MAX_END = [sum(m[0] <= b for m in MAXES) for b in range(NB)]
LEAD = NMAX - 2 * (NSTEP // 2)


def tower(nc, x, tok_table, op_table, var_table, const_table, struct_table, special_table,
          wq, wk, wv, wproj, q_w, k_w, omega, u,
          cn_w1, cn_b1, cn_w2, cn_b2, cn_w3, cn_b3, cn_w4, cn_b4,
          gc_w1, gc_b1, gc_w2, gc_b2, gc_w3, gc_b3, ada, out):
    nc.disable_value_cache = True
    ctx = ExitStack()
    with ctx:
        def sb(name, shape, dt, where=ctx):
            return where.enter_context(nc.sbuf_tensor(name, shape, dt))

        def sem(name):
            return ctx.enter_context(nc.semaphore(name))

        small_d = nc.dram_tensor("small_d", [NSMALL, HALF], F32).ap()
        qT_d = nc.dram_tensor("qT_d", [H, P, T], F16).ap()
        kT_d = nc.dram_tensor("kT_d", [H, P, T], F16).ap()
        v_d = nc.dram_tensor("v_d", [T, H * D], F32).ap()
        c_d = nc.dram_tensor("c_d", [NC * H, T], F16).ap()

        E = sb("E", [P, NT, C], F32)
        ident = sb("ident", [P, P], F32)
        ident16 = sb("ident16", [P, P], F16)
        identb = sb("identb", [P, P], BF16)
        mask_s = sb("mask_s", [P, P], BF16)
        mask_m = sb("mask_m", [P, BLK], F32)
        eps_t = sb("eps_t", [P, 1], F32)
        slope = sb("slope", [P, H], F32)
        off_i = sb("off_i", [P, NSTEP], I32)
        off = sb("off", [P, NSTEP], F32)
        BT = sb("BT", [P, H, NSTEP], F32)
        A1 = sb("A1", [P, 2, 2, T], F16)
        B1 = sb("B1", [P, 2, T], F16)
        BM = sb("BM", [P, 2, T], F16)
        wph = sb("wph", [P, NP, C], F32R)
        wpl = sb("wpl", [P, NP, C], F32R)

        pre = ExitStack()
        ids = sb("ids", [P, NT], I32, pre)
        far = sb("far", [P, NT], F32, pre)
        spec_ids = sb("spec_ids", [P, NT], I32, pre)
        wh = sb("wh", [P, 2, 3, H * D], F32R, pre)
        wl = sb("wl", [P, 2, 3, H * D], F32R, pre)
        wgf = sb("wgf", [P, 2, H], F32, pre)
        wg = sb("wg", [P, 2, 2, H], F32R, pre)
        graw = sb("graw", [P, 2, H], F32, pre)
        GP = sb("GP", [P, NT, 2, H], F32, pre)
        qwb = sb("qwb", [P, D], F32, pre)
        kwb = sb("kwb", [P, D], F32, pre)
        wqk = sb("wqk", [P, D], F32, pre)
        un = sb("un", [P, H], F32, pre)
        bn6 = sb("bn6", [P, 2, 6], F32, pre)
        mv = sb("mv", [P, 2, 2], F32, pre)
        ls = sb("ls", [P, 2, 1], F32, pre)
        lr = sb("lr", [P, 2, 1], F32, pre)
        XN = sb("XN", [P, 2, C], F32, pre)
        XH = sb("XH", [P, 2, 2, P], F32R, pre)
        XL = sb("XL", [P, 2, 2, P], F32R, pre)
        SQ = sb("SQ", [P, 2 * H, D], F32, pre)
        ms = sb("ms", [P, 2 * H], F32, pre)
        sr = sb("sr", [P, 2 * H], F32, pre)
        rr = sb("rr", [P, 2 * H], F32, pre)
        QN = sb("QN", [P, H, D], F32, pre)
        KN = sb("KN", [P, H, D], F32, pre)
        tmp, ub = QN, KN
        KW = sb("KW", [P, H, D], F32, pre)
        QT = sb("QT", [P, 2, H, P], F16, pre)
        KT = sb("KT", [P, 2, H, P], F16, pre)
        VS = sb("VS", [P, 2, H * D], F32, pre)
        STQ = sb("STQ", [P, H, 2 * P], F16, pre)
        STK = sb("STK", [P, H, 2 * P], F16, pre)
        GL = sb("GL", [P, NT + 1, H], F32, pre)
        na = sb("na", [P, NT + 1, H], F32, pre)
        sp = sb("sp", [P, NT + 1, H], F32, pre)
        early = ExitStack()
        wst = sb("wst", [P, WST, H * D], F32, early)
        wp = wst[:, 0:2, :].rearrange("p a (b n) -> p (a b) n", n=C)
        early.close()
        cw = sb("cw", [P, H], F32, pre)
        cc = sb("cc", [P, NT, H], F32, pre)
        rest = sb("rest", [P, NT, H], F32, pre)
        CP = sb("CP", [P, NT, H, NC], F16, pre)
        jc = sb("jc", [P, NT, H], F32, pre)
        at_j = sb("at_j", [P, NT], F32, pre)
        CT = sb("CT", [NC * H, T], F16, pre)
        pre.close()

        ot = ExitStack()
        OT = sb("OT", [P, NP, T], F32, ot)
        att = ExitStack()
        A2 = sb("A2", [P, 2, T], F16, att)
        B2 = sb("B2", [P, 2, T], F16, att)
        V = sb("V", [P, NT, P], F32, att)
        PB = sb("PB", [P, P_RING, BLK], F32, att)
        acc = sb("acc", [P, 2, 2, BLK], F32, att)
        lnr = sb("lnr", [P, BLK], F32, att)
        R = sb("R", [P, BLK], F32, att)
        bts = sb("bts", [P, 2, 2, NSTEP], F32, att)
        mxp = sb("mxp", [P, 2, NB, 2 * TPB, NB], F32, att)
        nmf = sb("nmf", [P, 2, TPB, 2], F32, att)
        nm = sb("nm", [P, 2, 2, TPB], F16, att)
        carry = sb("carry", [P, NMAX], F32, att)
        mrow = sb("mrow", [2 * 2 * TPB, P], F16, att)
        ones = sb("ones", [P, D], F32, att)
        att.close()

        ot.close()
        room = NP * T * 4
        TH = sb("TH", [P, 2, T], F32R)
        TL = sb("TL", [P, 2, T], F32R)
        h1 = sb("h1", [P, 2, BLK], F32)
        h1h = sb("h1h", [P, 2, BLK], F32R)
        h1l = sb("h1l", [P, 2, BLK], F32R)
        h2 = sb("h2", [P, BLK], F32)
        h3 = sb("h3", [P, BLK], F32)
        th = sb("th", [P, BLK], F32)
        cp = sb("cp", [P, BLK], F32)
        du = sb("du", [P, BLK], F32)
        dw = sb("dw", [P, BLK], F32)
        room -= 2 * 2 * T * 4 + (3 * 2 + 6) * BLK * 4
        sb("rest_of_ot", [P, room // 4], F32)
        TT = sb("TT", [P, 2, T], F32)
        X2 = sb("X2", [P, 2, C], F32)
        OH = sb("OH", [P, 2, NP, P], F32R)
        OL = sb("OL", [P, 2, NP, P], F32R)
        bn6b = sb("bn6b", [P, 2, 6], F32)
        mvb = sb("mvb", [P, 2, 2], F32)
        lsb = sb("lsb", [P, 2, 1], F32)
        lrb = sb("lrb", [P, 2, 1], F32)
        gm = sb("gm", [P, 2, NT], F32)
        gmean = sb("gmean", [P, 2], F32)
        gv = sb("gv", [P, 4], F32)
        w1 = sb("w1", [P, 2, C], F32)
        w2 = sb("w2", [P, 2, P], F32)
        w1h = sb("w1h", [P, 2, C], F32R)
        w1l = sb("w1l", [P, 2, C], F32R)
        w2h = sb("w2h", [P, 2, P], F32R)
        w2l = sb("w2l", [P, 2, P], F32R)
        w3 = sb("w3", [P, P], F32)
        w4c = sb("w4c", [P, 1], F32)
        w4 = sb("w4", [P, P], F32)
        gw1 = sb("gw1", [P, 2, P], F32)
        gw2 = sb("gw2", [P, P], F32)
        gw3c = sb("gw3c", [P, 1], F32)
        gw3 = sb("gw3", [P, P], F32)
        bias = sb("bias", [P, 9], F32)
        halfb = sb("halfb", [P, 2], F32)
        sgn = sb("sgn", [P, 1], F32)
        cpl = sb("cpl", [P, 2], F32)

        PS = ctx.enter_context(nc.psum_tensor("PS", [P, 8, 512], F32))

        def bank(n):
            return PS[:, n, :]

        QB, KB, VB = PS[:, 0:2, :], PS[:, 2:4, :], PS[:, 4:6, :]
        TA, TB = 6, 7

        ld_ids, ld_small, ld_small2, ld_small3, ld_small4 = (sem(n) for n in ("ld_ids", "ld_small", "ld_small2", "ld_small3", "ld_small4"))
        ld_w = [sem(f"ld_w{i}") for i in range(6)]
        ld_u, ld_wp, wph_ready, wp_split = sem("ld_u"), sem("ld_wp"), sem("wph_ready"), sem("wp_split")
        oh_ready, ol_ready = sem("oh_ready"), sem("ol_ready")
        idx_ready = sem("idx_ready")
        tok_in, spec_in = sem("tok_in"), sem("spec_in")
        small_in = [sem("small_in0"), sem("small_in1")]
        consts = sem("consts")
        wh_ready, w_split = sem("wh_ready"), sem("w_split")
        u_sq, u_norm = sem("u_sq"), sem("u_norm")
        dv, pl, ac = sem("dve_chain"), sem("pool_chain"), sem("act_chain")
        bn_ready, ln_sqrt, xn_ready, xt_done = sem("bn_ready"), sem("ln_sqrt"), sem("xn_ready"), sem("xt_done")
        xh_ready, xl_ready = sem("xh_ready"), sem("xl_ready")
        q_done, k_done, v_done, g_done = sem("q_done"), sem("k_done"), sem("v_done"), sem("g_done")
        sqq_ready, sqk_ready, redq_done, redk_done, sr_ready = (sem(n) for n in ("sqq_ready", "sqk_ready", "redq_done", "redk_done", "sr_ready"))
        qn_ready, kn_ready, kw_ready = sem("qn_ready"), sem("kn_ready"), sem("kw_ready")
        q_high, q_low, k_high, k_low = sem("q_high"), sem("q_low"), sem("k_high"), sem("k_low")
        trq_done, trk_done, stq_filled, stk_filled = sem("trq_done"), sem("trk_done"), sem("stq_filled"), sem("stk_filled")
        v_copied, g_read, gl_ready = sem("v_copied"), sem("g_read"), sem("gl_ready")
        v_stored = [sem("v_stored0"), sem("v_stored1")]
        q_stored, k_stored, c_stored = sem("q_stored"), sem("k_stored"), sem("c_stored")
        sp_neg, sp_exp, sp_ln, cp_ready, ct_done, ct_copied, bt_ready = (sem(n) for n in ("sp_neg", "sp_exp", "sp_ln", "cp_ready", "ct_done", "ct_copied", "bt_ready"))

        rows_set = sem("rows_set")
        ld_a1 = [sem("ld_a1_0"), sem("ld_a1_1")]
        ld_bm = [sem(f"ld_bm_{c}") for c in range(NB)]
        ld_a2 = [sem(f"ld_a2_{c}") for c in range(NB)]
        ld_b = [sem(f"ld_b_{c}") for c in range(NB)]
        ld_v = [sem(f"ld_v_{c}") for c in range(NB)]
        s_done, exp_done, pv_done = sem("s_done"), sem("exp_done"), sem("pv_done")
        sums = [sem("sums_a"), sem("sums_b")]
        mx_done, mx_read = sem("mx_done"), sem("mx_read")
        nm_ready, mrow_in = sem("nm_ready"), sem("mrow_in")
        misc_done, misc_read = sem("misc_done"), sem("misc_read")
        r_ready, o_done = sem("r_ready"), sem("o_done")

        ffz, ld_ff, ff_set = sem("ffz"), sem("ld_ff"), sem("ff_set")
        proj_done, h_added, bn2_ready, ln2_sqrt = sem("proj_done"), sem("h_added"), sem("bn2_ready"), sem("ln2_sqrt")
        x2_ready, x2t_done, tt_copied = sem("x2_ready"), sem("x2t_done"), sem("tt_copied")
        gmean_ready, g_mm, g_act, cpl_ready = sem("gmean_ready"), sem("g_mm"), sem("g_act"), sem("cpl_ready")
        l_done = [sem(f"l{i}_done") for i in range(1, 5)]
        a_done = [sem(f"a{i}_done") for i in range(1, 5)]
        dw_ready, t0_new, t1_new = sem("dw_ready"), sem("t0_new"), sem("t1_new")
        out_t, out_sum, out_stored = sem("out_t"), sem("out_sum"), sem("out_stored")
        wsplit2, th_ready = sem("wsplit2"), sem("th_ready")
        tl_ready = [sem("tl0_ready"), sem("tl1_ready")]
        h1h_ready = sem("h1h_ready")
        h1l_ready = sem("h1l_ready")
        att_over, ff_dve, cp_made, du_ready = sem("att_over"), sem("ff_dve"), sem("cp_made"), sem("du_ready")

        class Chain:

            def __init__(self, s):
                self.s, self.base, self.n = s, 0, 0

            def inc(self, ins):
                ins.then_inc(self.s, 1)
                self.n += 1

            def wait(self, eng):
                eng.wait_ge(self.s, self.base + self.n)

        def tiles(eng, step, per_chain=None, chain=None):
            for t in range(2):
                step(t, t, 0)
            if chain is not None:
                base = chain.base + chain.n
                start = chain.n
                chain.n = 0
            with eng.Fori(1, NT // 2 - 1) as n:
                if chain is not None:
                    chain.base = (n - 1) * (2 * per_chain) + base
                step(n * 2, 0, n)
                step(n * 2 + 1, 1, n)
            if chain is not None:
                assert chain.n == 2 * per_chain, chain.n
                chain.base, chain.n = base + (NT - 4) * per_chain, 0
            for t in range(NT - 2, NT):
                step(t, t % 2, t // 2)

        def s_bank(unit):
            return bank(unit % S_RING)

        def bank_before(unit):
            return next(u for u in range(unit - 1, -2 * PER_BODY, -1) if u % (2 * PER_BODY) % S_RING == unit % S_RING)

        def mx_bank(m):
            return bank(3 + m % MX_RING)

        def o_bank(b):
            return bank(5 + b % 2)

        MISC = 7
        PER_BODY = 2 * NSTEP
        T_AT = {4: (2,), 20: (3,), 32: (0, 1)}
        BLOCK_END = [BIAS_AT[b] + block_tiles(b) for b in range(NB)]
        MISC_USES = []
        for k in range(PER_BODY):
            par, s_ = divmod(k, NSTEP)
            for b in range(NB):
                if BLOCK_END[b] + 3 == s_:
                    MISC_USES.append((k, "sums", par, b))
            if s_ == 3:
                MISC_USES.append((k, "sums", par - 1, NB - 1))
            if s_ - 1 in T_AT:
                MISC_USES.append((k, "row", par, T_AT[s_ - 1]))
        NMISC = len(MISC_USES)
        LAST = NP // 2 - 1

        def misc_at(iv, k):
            out = []
            for i, (at, kind, par, what) in enumerate(MISC_USES):
                before_all = isinstance(iv, int) and iv == 0 and par < 0
                no_next = isinstance(iv, int) and iv == LAST and kind == "row" and what == (0, 1) and par == 1
                if at == k and not before_all and not no_next:
                    out.append((i, kind, par, what))
            return out

        def row_index(par, blocks):
            return next(i for i, use in enumerate(MISC_USES) if use[1:] == ("row", par, blocks))

        def sums_done(iv, par, b):
            if par < 0 and b < NB - 1:
                return iv * NMISC + (next(i for i, use in enumerate(MISC_USES) if use[1:] == ("sums", 1, b)) - NMISC + 2)
            return iv * NMISC + (next(i for i, use in enumerate(MISC_USES) if use[1:] == ("sums", par, b)) + 2)

        FIRST = P_RING // 2

        def bodies(e, steps):
            steps(0, 0, FIRST)
            with e.Fori(0, LAST) as iv:
                steps(iv, FIRST, PER_BODY)
                steps(iv + 1, 0, FIRST)
            steps(LAST, FIRST, PER_BODY)

        def max_units(iv, k):
            par, s_ = divmod(k, NSTEP)
            for j in range(2):
                m = LEAD + 2 * s_ + j
                if isinstance(iv, int) and iv == LAST and par + m // NMAX > 1:
                    return
                yield NMAX * par + m, (par + m // NMAX) % 2, m % NMAX

        BLOCK_STARTS = [0] + MAX_END[:-1]

        def max_shape(m):
            b, qt, hd, c = MAXES[m]
            return b, qt, hd, c, (P * (qt + 1) if c == b else BLK)

        block = ctx.enter_context(nc.Block())

        def add_up(e, eng, iv, k, hd):
            par, s_ = divmod(k, NSTEP)
            b, j = STEPS[s_]
            c0 = P * max(j - TPB * b, 0)
            done = iv * PER_BODY + k
            src = PB[:, (2 * k + hd) % P_RING, c0:]
            dst = acc[:, b % 2, hd, c0:]
            e.wait_ge(exp_done, done * 2 + hd + 1)
            if j == 0:
                if not (isinstance(iv, int) and iv == 0 and par == 0 and b < 2):
                    e.wait_ge(misc_done, sums_done(iv, par, b - 2) if b >= 2 else sums_done(iv, par - 1, b + 2))
                eng.tensor_tensor(dst, src, ones[:, 0:1].broadcast_to([P, BLK]), ALU.mult).then_inc(sums[hd], 1)
            else:
                e.wait_ge(sums[hd], done)
                eng.tensor_tensor(dst, dst, src, ALU.add).then_inc(sums[hd], 1)

        NCONST = 3 + 2 + H + NB

        @block.sync
        def _(sp_):
            e = sp_
            e.dma_start(ids[:, :], x.rearrange("o (t p) -> p (o t)", p=P), allow_slow_non_contiguous=True).then_inc(ld_ids, 16)
            for i, (tab, s) in enumerate(((op_table, ld_small), (var_table, ld_small2), (const_table, ld_small3), (struct_table, ld_small4))):
                e.dma_start(small_d[SMALL * i:SMALL * (i + 1), :], tab).then_inc(s, 16)
            e.dma_start(ub[:, :, :].rearrange("p h d -> p (h d)"),
                        u.rearrange("h d -> (h d)").rearrange("(o n) -> o n", o=1).broadcast_to([P, H * D])).then_inc(ld_u, 16)
            for dst, src in ((qwb, q_w), (kwb, k_w), (GL[:, NT, :], omega)):
                n = src.shape[0]
                dst = dst[:, :] if dst is qwb or dst is kwb else dst
                e.dma_start(dst, src.rearrange("(o n) -> o n", o=1).broadcast_to([P, n])).then_inc(ld_u, 16)
            n = 0
            for m, w in enumerate((wq, wk, wv)):
                for half in range(2):
                    if n >= WST:
                        e.wait_ge(w_split, n - WST + 1)
                    e.dma_start(wst[:, n % WST, :], w[P * half:P * (half + 1), :]).then_inc(ld_w[n], 16)
                    n += 1
            e.wait_ge(w_split, 6)
            e.dma_start(wp, wproj.rearrange("(a p) n -> p a n", p=P)).then_inc(ld_wp, 16)

            def store(t, r, n):
                at_least(e, v_copied, t + 1)
                e.dma_start(v_d[bass.ds(t * P, P), :], VS[:, r, :]).then_inc(v_stored[r], 16)
                if r == 0 and not (isinstance(t, int) and t == 0):
                    stage(n - 1)

            def stage(n):
                e.wait_ge(stq_filled, n * 4 + 4)
                e.dma_start(qT_d[:, :, bass.ds(n * (2 * P), 2 * P)].rearrange("h r t -> r h t"), STQ[:, :, :]).then_inc(q_stored, 16)
                e.wait_ge(stk_filled, n * 4 + 4)
                e.dma_start(kT_d[:, :, bass.ds(n * (2 * P), 2 * P)].rearrange("h r t -> r h t"), STK[:, :, :]).then_inc(k_stored, 16)

            tiles(e, store)
            stage(NT // 2 - 1)
            e.wait_ge(ct_copied, 2)
            e.dma_start(c_d, CT[:, :]).then_inc(c_stored, 16)
            e.wait_ge(c_stored, 16)
            for r in range(2):
                e.wait_ge(v_stored[r], 16 * (NT // 2))
            e.wait_ge(q_stored, 16 * (NT // 2))
            e.wait_ge(k_stored, 16 * (NT // 2))
            e.wait_ge(bt_ready, NB)
            e.wait_ge(rows_set, 9)
            e.wait_ge(wp_split, 2)

            def chunk(c):
                return slice(BLK * c, BLK * (c + 1))

            def load_a1(q, r):
                e.dma_start(A1[0:D, r, :, :], kT_d[bass.ds(q * 2, 2), 0:D, :].rearrange("h r t -> r h t")).then_inc(ld_a1[r], 16)
                e.dma_start(A1[D:D + NC, r, :, :], c_d.rearrange("(h k) t -> k h t", k=NC)[:, bass.ds(q * 2, 2), :]).then_inc(ld_a1[r], 16)

            def high_queries(dst, q, c, s):
                e.dma_start(dst[0:D, :, chunk(c)], qT_d[bass.ds(q * 2, 2), D:P, chunk(c)].rearrange("h r t -> r h t")).then_inc(s, 16)

            def load_b(q, c):
                high_queries(B1, q, c, ld_b[c])
                e.dma_start(B2[:, :, chunk(c)], qT_d[bass.ds(q * 2, 2), :, chunk(c)].rearrange("h r t -> r h t")).then_inc(ld_b[c], 16)

            def load_kv(q, c):
                e.dma_start(A2[:, :, chunk(c)], kT_d[bass.ds(q * 2, 2), :, chunk(c)].rearrange("h r t -> r h t")).then_inc(ld_a2[c], 16)
                e.dma_start(V[:, TPB * c:TPB * (c + 1), :],
                            v_d[chunk(c), bass.ds(q * P, P)].rearrange("(j p) n -> p j n", p=P)).then_inc(ld_v[c], 16)

            def load_rows(blocks, count):
                e.wait_ge(misc_read, count)
                for i, b in enumerate(blocks):
                    for hd in range(2):
                        at = 2 * TPB * i + TPB * hd
                        e.dma_start(B1[MAX_ROW:MAX_ROW + 1, hd, chunk(b)], mrow[at:at + TPB, :]).then_inc(mrow_in, 16)

            load_a1(0, 0)
            for c in range(NB):
                high_queries(BM, 0, c, ld_bm[c])
            for c in range(NB):
                load_b(0, c)
                load_kv(0, c)
            load_rows((0, 1), 2)

            def pair_loads(iv, par):
                q = iv * 2 + par
                more = not (isinstance(iv, int) and par == 1)
                nxt = q + 1
                if more:
                    e.wait_ge(pv_done, q * NSTEP + 1)
                    load_a1(nxt, 1 - par)
                    for c in (0, 1):
                        high_queries(BM, nxt, c, ld_bm[c])
                for b in range(NB - 1):
                    if more:
                        e.wait_ge(s_done, q * (2 * NSTEP) + 2 * BLOCK_END[b])
                        load_b(nxt, b)
                    if b < 2:
                        load_rows((b + 2,), iv * NMISC + row_index(par, (b + 2,)) + 2)
                        if more:
                            e.wait_ge(mx_done, q * NMAX + MAX_END[b + 2])
                            high_queries(BM, nxt, b + 2, ld_bm[b + 2])
                if more:
                    for c in range(NB):
                        e.wait_ge(pv_done, q * NSTEP + BIAS_AT[NB - 1] + TPB * (c + 1))
                        load_kv(nxt, c)
                        if c == 1:
                            load_rows((0, 1), iv * NMISC + row_index(par, (0, 1)) + 2)
                    load_b(nxt, NB - 1)

            with e.Fori(0, LAST) as iv:
                pair_loads(iv, 0)
                pair_loads(iv, 1)
            pair_loads(LAST, 0)
            pair_loads(LAST, 1)
            e.wait_ge(o_done, 2 + NB * NP)
            e.nop().then_inc(att_over, 1)
            e.wait_ge(ffz, 5)
            loads = [(w1[:, :, :], cn_w1.rearrange("(a p) n -> p a n", p=P)), (w2[:, :, :], cn_w2.rearrange("(a p) n -> p a n", p=P)),
                     (w3[:, 0:D], cn_w3), (w4c[0:D, :], cn_w4), (gw1[:, :, :], gc_w1.rearrange("(a p) n -> p a n", p=P)),
                     (gw2[:, 0:D], gc_w2), (gw3c[0:D, :], gc_w3)]
            for i, (b_, n) in enumerate(((cn_b1[0:P], P), (cn_b1[P:C], P), (cn_b2, P), (cn_b3, D), (cn_b4, 0), (gc_b1, P), (gc_b2, D), (gc_b3, 0), (ada, 0))):
                src = b_.rearrange("(p o) -> p o", o=1) if n else b_.rearrange("(o n) -> o n", o=1).broadcast_to([P, 1])
                loads.append((bias[0:(n or P), i:i + 1], src))
            assert len(loads) == FF_LOADS
            for dst, src in loads:
                e.dma_start(dst, src).then_inc(ld_ff, 16)
            for b in range(NB):
                e.wait_ge(out_sum, 2 * (b + 1))
                e.dma_start(out[BLK * b:BLK * (b + 1), :].rearrange("(t p) c -> p t c", p=P), E[:, TPB * b:TPB * (b + 1), :]).then_inc(out_stored, 16)
            e.wait_ge(out_stored, 16 * NB)

        @block.gpsimd
        def _(e):
            g = nc.gpsimd
            ch = Chain(pl)
            ch.inc(g.memset(ident[:, :], 1.0))
            ch.wait(e)
            ch.inc(g.affine_select(out=ident[:, :], in_=ident[:, :], compare_op=ALU.is_equal, fill=0.0,
                                   base=0, pattern=[[-1, P]], channel_multiplier=1))
            ch.wait(e)
            g.memset(eps_t[:, :], EPS).then_inc(consts, 1)
            g.tensor_copy(ident16[:, :], ident[:, :]).then_inc(consts, 1)
            g.tensor_copy(identb[:, :], ident[:, :]).then_inc(consts, 1)
            e.wait_ge(ld_ids, 16)
            e.wait_ge(idx_ready, 1)
            for s in (ld_small, ld_small2, ld_small3, ld_small4):
                e.wait_ge(s, 16)

            def idx(a, t):
                return bass.IndirectOffsetOnAxis(ap=a[:, t:t + 1].bitcast(U32), axis=0)

            def gather(t):
                e.indirect_dma_start(E[:, t, 0:HALF], None, tok_table, idx(ids, t)).then_inc(tok_in, 16)
                e.indirect_dma_start(E[:, t, HALF:C], None, special_table, idx(spec_ids, t),
                                     bounds_check=special_table.shape[0] - 1, oob_is_err=False).then_inc(spec_in, 16)

            def gather_small(t):
                e.wait_ge(tok_in, 16 * (t + 1))
                e.wait_ge(spec_in, 16 * (t + 1))
                e.indirect_dma_start(E[:, t, HALF:C], None, small_d, idx(ids, t),
                                     bounds_check=NSMALL - 1, oob_is_err=False).then_inc(small_in[t % 2], 16)

            gather(0)
            gather_small(0)
            gather(1)
            gather_small(1)
            for t in (2, 3):
                gather(t)
                e.wait_ge(small_in[t % 2], 16)
                gather_small(t)
            ch.inc(g.memset(mask_s[:, :], 0.0))
            ch.inc(g.memset(mask_m[:, :], 0.0))
            ch.wait(e)
            g.affine_select(out=mask_s[:, :], in_=mask_s[:, :], compare_op=ALU.is_ge, fill=NEG,
                            base=0, pattern=[[1, P]], channel_multiplier=-1).then_inc(consts, 1)
            g.affine_select(out=mask_m[:, BLK - P:], in_=mask_m[:, BLK - P:], compare_op=ALU.is_ge, fill=NEG,
                            base=0, pattern=[[-1, P]], channel_multiplier=1).then_inc(consts, 1)
            for h in range(H):
                g.memset(slope[:, h:h + 1], 2.0 ** (-0.5 * (h + 1))).then_inc(consts, 1)
            for b in range(NB):
                n = block_tiles(b)
                g.iota(off_i[:, BIAS_AT[b]:BIAS_AT[b] + n], pattern=[[P, n]], base=-BLK * b, channel_multiplier=1).then_inc(consts, 1)
            def set_rows(count, what):
                what().then_inc(rows_set, 1)
                e.wait_ge(rows_set, count + 1)

            def ramp(dst, pattern):
                return g.iota(dst, pattern=pattern, base=0, channel_multiplier=0, allow_small_or_imprecise_dtypes=True)

            e.wait_ge(consts, NCONST)
            set_rows(0, lambda: g.memset(A1[96:P, :, :, :], 8.0))
            rows = {
                1: (1, lambda: g.memset(B1[D:P, :, :], 0.0)),
                2: (2, lambda: g.memset(BM[D:P, :, :], 0.0)),
                3: (3, lambda: ramp(B1[D:D + 3, 0, :], [[0, NB], [1, BLK]])),
                4: (4, lambda: ramp(B1[D:D + 3, 1, :], [[0, NB], [1, BLK]])),
                5: (5, lambda: g.memset(BM[D:D + NC, :, :], 64.0)),
                6: (6, lambda: ramp(BM[D:D + 3, 0, :], [[1, T]])),
                7: (7, lambda: ramp(BM[D:D + 3, 1, :], [[1, T]])),
                12: (8, lambda: g.memset(A1[D:MAX_ROW, :, :, :], 0.0)),
            }
            for t in range(NT):
                r = t % 2
                if t + 4 < NT:
                    gather(t + 4)
                e.wait_ge(kn_ready, t + 1)
                at_least(e, k_low, t)
                g.tensor_tensor(KW[:, :, :], KN[:, :, :],
                                wqk[:, :].rearrange("p (o d) -> p o d", o=1).broadcast_to([P, H, D]), ALU.mult).then_inc(kw_ready, 1)
                if t + 4 < NT:
                    gather_small(t + 4)
                e.wait_ge(k_high, t + 1)
                g.tensor_tensor(KT[:, r, :, D:P], KW[:, :, :], KT[:, r, :, 0:D], ALU.subtract).then_inc(k_low, 1)
                if t in (8, 9):
                    half = slice(4 * (t - 8), 4 * (t - 7))
                    e.wait_ge(wph_ready, 1)
                    g.tensor_tensor(wpl[:, half, :], wp[:, half, :], wph[:, half, :].bitcast(F32), ALU.subtract).then_inc(wp_split, 1)
                if t in rows:
                    e.wait_ge(k_low, t + 1)
                    set_rows(*rows[t])
            e.wait_ge(o_done, 2)
            def steps(iv, first, end):
                for k in range(first, end):
                    add_up(e, g, iv, k, 1)

            bodies(e, steps)
            e.wait_ge(att_over, 1)
            for z in (w3, w4, gw2, gw3, bias):
                g.memset(z[:, :], 0.0).then_inc(ffz, 1)
            g.memset(sgn[:, :], 1.0).then_inc(ffz, 1)
            e.wait_ge(ffz, 6)
            g.memset(sgn[D:P, :], -1.0).then_inc(ffz, 1)

            e.wait_ge(ffz, 7)
            e.wait_ge(ld_ff, FF_LOADS * 16)
            for i, (w, wh_, wl_) in enumerate(((w1, w1h, w1l), (w2, w2h, w2l))):
                g.tensor_copy(wh_[:, :, :], w[:, :, :]).then_inc(wsplit2, 1)
                e.wait_ge(wsplit2, 2 * i + 1)
                g.tensor_tensor(wl_[:, :, :], w[:, :, :], wh_[:, :, :].bitcast(F32), ALU.subtract).then_inc(wsplit2, 1)

            def low1(n, b):
                e.wait_ge(th_ready, n * 2 + 2)
                sl = slice(BLK * b, BLK * (b + 1))
                g.tensor_tensor(TL[:, 1, sl], TT[:, 1, sl], TH[:, 1, sl].bitcast(F32), ALU.subtract).then_inc(tl_ready[1], 1)

            def update(n, b):
                e.wait_ge(dw_ready, n + 1)
                sl = slice(BLK * b, BLK * (b + 1))
                g.tensor_tensor(TT[:, 1, sl], TT[:, 1, sl], dw[:, :], ALU.subtract).then_inc(t1_new, 1)

            for b in range(NB):
                low1(b, b)
            with e.Fori(0, CYCLES - 1) as cyc:
                for b in range(NB):
                    update(cyc * NB + b, b)
                    low1(cyc * NB + (NB + b), b)
            for b in range(NB):
                update((CYCLES - 1) * NB + b, b)
                if b == 0:
                    low1(CYCLES * NB, b)

        @block.scalar
        def _(e):
            a = nc.scalar
            for n in range(6):
                e.wait_ge(ld_w[n], 16)
                a.activation(wh[:, n % 2, n // 2, :], wst[:, n % WST, :], ACT.Copy).then_inc(wh_ready, 1)
                if n == 1:
                    e.wait_ge(consts, 3)
                    e.wait_ge(u_sq, 1)
                    a.activation(un[:, :], un[:, :], ACT.Sqrt).then_inc(u_norm, 1)
                    e.wait_ge(bn_ready, 1)
                    a.activation(ls[:, 0, :], mv[:, 0, 1:2], ACT.Sqrt, bias=eps_t[:, 0:1]).then_inc(ln_sqrt, 1)
                    e.wait_ge(xt_done, 1)
                    a.activation(XH[:, 0, :, :].rearrange("p a n -> p (a n)"), bank(TA)[:, C:2 * C], ACT.Copy).then_inc(xh_ready, 1)
                if n == 3:
                    e.wait_ge(bn_ready, 2)
                    a.activation(ls[:, 1, :], mv[:, 1, 1:2], ACT.Sqrt, bias=eps_t[:, 0:1]).then_inc(ln_sqrt, 1)

            def evac_q(t, r, n, k):
                e.wait_ge(trq_done, t * 2 + k + 1)
                if k == 0 and r == 0:
                    at_least(e, q_stored, n * 16)
                a.activation(STQ[:, 8 * k:8 * k + 8, P * r:P * (r + 1)],
                             bank((TB, TA)[k]).bitcast(F16).rearrange("p (h n) -> p h n", n=P), ACT.Copy).then_inc(stq_filled, 1)

            def keys_high(t, r):
                e.wait_ge(kw_ready, t + 1)
                a.activation(KT[:, r, :, 0:D], KW[:, :, :], ACT.Copy).then_inc(k_high, 1)

            def step(t, r, n):
                first, last = isinstance(t, int) and t == 0, isinstance(t, int) and t == NT - 1
                near_end = isinstance(t, int) and t >= NT - 2
                n_before = n - 1 if r == 0 else n
                if not first:
                    keys_high(t - 1, 1 - r)
                e.wait_ge(q_done, t + 1)
                at_least(e, redq_done, t)
                a.activation(SQ[:, 0:H, :].rearrange("p h d -> p (h d)"), QB.rearrange("p a n -> p (a n)"), ACT.Square).then_inc(sqq_ready, 1)
                e.wait_ge(k_done, t + 1)
                at_least(e, redk_done, t)
                a.activation(SQ[:, H:, :].rearrange("p h d -> p (h d)"), KB.rearrange("p a n -> p (a n)"), ACT.Square).then_inc(sqk_ready, 1)
                if not last:
                    e.wait_ge(xt_done, t + 2)
                    a.activation(XH[:, 1 - r, :, :].rearrange("p a n -> p (a n)"), bank(TA)[:, C:2 * C], ACT.Copy).then_inc(xh_ready, 1)
                if not first:
                    evac_q(t - 1, 1 - r, n_before, 0)
                e.wait_ge(redk_done, t + 1)
                a.activation(sr[:, :], ms[:, :], ACT.Sqrt, bias=eps_t[:, 0:1], scale=1.0 / D).then_inc(sr_ready, 1)
                if not near_end:
                    e.wait_ge(bn_ready, t + 3)
                    a.activation(ls[:, r, :], mv[:, r, 1:2], ACT.Sqrt, bias=eps_t[:, 0:1]).then_inc(ln_sqrt, 1)
                if not first:
                    evac_q(t - 1, 1 - r, n_before, 1)
                e.wait_ge(qn_ready, t + 1)
                a.activation(QT[:, r, :, D:P], QN[:, :, :], ACT.Copy).then_inc(q_high, 1)
                if isinstance(t, int) and t == 1:
                    e.wait_ge(ld_wp, 16)
                    a.activation(wph[:, :, :], wp, ACT.Copy).then_inc(wph_ready, 1)
                e.wait_ge(v_done, t + 1)
                at_least(e, v_stored[r], n * 16)
                a.activation(VS[:, r, :], VB.rearrange("p a n -> p (a n)"), ACT.Copy).then_inc(v_copied, 1)

            tiles(e, step)
            a.preload_act_table_set(EXP_LN_SET)
            e.wait_ge(sp_neg, 1)
            a.activation(na[:, :, :], na[:, :, :], ACT.Exp).then_inc(sp_exp, 1)
            e.wait_ge(sp_exp, 1)
            a.activation(na[:, :, :], na[:, :, :], ACT.Ln, bias=1.0).then_inc(sp_ln, 1)
            keys_high(NT - 1, 1)
            evac_q(NT - 1, 1, NT // 2 - 1, 0)
            evac_q(NT - 1, 1, NT // 2 - 1, 1)
            for k, tb in enumerate((TA, TB)):
                e.wait_ge(ct_done, k + 1)
                a.activation(CT[:, 1024 * k:1024 * (k + 1)], bank(tb)[0:NC * H, :].bitcast(F16), ACT.Copy).then_inc(ct_copied, 1)

            def row(n, count):
                e.wait_ge(misc_done, count)
                return a.activation(mrow[0:n, :], bank(MISC)[0:n, 0:P // 2].bitcast(F16), ACT.Copy)

            e.wait_ge(bt_ready, NB)
            row(2 * 2 * TPB, 2).then_inc(misc_read, 2)

            def misc(i, kind, iv, upar, what):
                if kind == "row":
                    before = {(2,): 64, (3,): 96, (0, 1): 128}[what]
                    e.wait_ge(mrow_in, iv * 256 + (128 * upar + before))
                    row(2 * TPB * len(what), iv * NMISC + (i + 2)).then_inc(misc_read, 1)
                else:
                    e.wait_ge(misc_done, iv * NMISC + (i + 2))
                    a.activation(lnr[:, :], bank(MISC), ACT.Ln).then_inc(misc_read, 1)
                    e.wait_ge(misc_read, iv * NMISC + (i + 2))
                    e.wait_ge(o_done, iv * (2 * NB) + (NB * upar + what + 2))
                    a.activation(R[:, :], lnr[:, :], ACT.Exp, scale=-1.0).then_inc(r_ready, 1)

            def steps(iv, first, end):
                for k in range(first, end):
                    par, s_ = divmod(k, NSTEP)
                    b, j = STEPS[s_]
                    c0 = P * max(j - TPB * b, 0)
                    q = iv * 2 + par
                    if s_ == 0:
                        a.activation(bts[:, par, :, :], BT[:, bass.ds(q * 2, 2), :], ACT.Copy).then_inc(ac, 1)
                        e.wait_ge(ac, q + 1)
                    for hd in range(2):
                        unit = 2 * k + hd
                        e.wait_ge(s_done, iv * (2 * PER_BODY) + unit + 1)
                        at_least(e, pv_done, iv * PER_BODY + ((unit - P_RING) // 2 + 1))
                        at_least(e, sums[hd], iv * PER_BODY + ((unit - P_RING) // 2 + 1))
                        a.activation(PB[:, unit % P_RING, c0:], s_bank(unit)[:, c0:], ACT.Exp,
                                     bias=bts[:, par, hd, s_:s_ + 1], scale=0.125).then_inc(exp_done, 1)
                    for i, kind, upar, what in misc_at(iv, k):
                        misc(i, kind, iv, upar, what)

            bodies(e, steps)
            misc(-1, "sums", LAST + 1, -1, NB - 1)
            def transposed(t):
                for half in range(2):
                    e.wait_ge(x2t_done, t + 1)
                    a.activation(TT[:, half, P * t:P * (t + 1)], bank(2 + t % 2)[:, P * half:P * (half + 1)], ACT.Copy,
                                 accum_out=gm[:, half, t:t + 1]).then_inc(tt_copied, 1)

            def high(t):
                at_least(e, proj_done, t - 1)
                a.activation(OH[:, t % 2, :, :], OT[:, :, P * t:P * (t + 1)], ACT.Copy).then_inc(oh_ready, 1)

            e.wait_ge(att_over, 1)
            high(0)
            high(1)
            for t in range(NT):
                if t + 2 < NT:
                    high(t + 2)
                e.wait_ge(bn2_ready, t + 1)
                a.activation(lsb[:, t % 2, :], mvb[:, t % 2, 1:2], ACT.Sqrt, bias=eps_t[:, 0:1]).then_inc(ln2_sqrt, 1)
                if t >= 2:
                    transposed(t - 2)
            transposed(NT - 2)

            def context(i):
                f, b_, s = ((ACT.Gelu, bias[:, 5:6], 1.0), (ACT.Gelu, bias[:, 6:7], 1.0), (ACT.Tanh, halfb[:, 1:2], 0.5))[i]
                e.wait_ge(g_mm, i + 1)
                a.activation(gv[:, i:i + 1], bank(1)[:, 0:1], f, bias=b_, scale=s).then_inc(g_act, 1)

            def high1(n, b, half):
                sl = slice(BLK * b, BLK * (b + 1))
                if isinstance(n, int) and n < NB:
                    e.wait_ge(tt_copied, 2 * TPB * (b + 1))
                else:
                    e.wait_ge((t0_new, t1_new)[half], n - (NB - 1))
                a.activation(TH[:, half, sl], TT[:, half, sl], ACT.Copy).then_inc(th_ready, 1)

            def gelu1(n):
                for half in range(2):
                    e.wait_ge(l_done[0], n * 2 + half + 1)
                    at_least(e, h1l_ready, n * 2)
                    at_least(e, l_done[1], n)
                    a.activation(h1[:, half, :], bank(4 + half), ACT.Gelu, bias=bias[:, half:half + 1]).then_inc(a_done[0], 1)
                    a.activation(h1h[:, half, :], bank(4 + half), ACT.Gelu, bias=bias[:, half:half + 1]).then_inc(h1h_ready, 1)

            def gelu2(n):
                e.wait_ge(l_done[1], n + 1)
                at_least(e, l_done[2], n)
                a.activation(h2[:, :], bank(6), ACT.Gelu, bias=bias[:, 2:3]).then_inc(a_done[1], 1)

            def gelu3(n):
                e.wait_ge(l_done[2], n + 1)
                at_least(e, l_done[3], n)
                a.activation(h3[:, :], bank(7), ACT.Gelu, bias=bias[:, 3:4]).then_inc(a_done[2], 1)

            def tanh(n):
                e.wait_ge(l_done[3], n + 1)
                at_least(e, cp_made, n)
                a.activation(th[:, :], bank(0), ACT.Tanh, bias=halfb[:, 0:1], scale=0.5).then_inc(a_done[3], 1)

            e.wait_ge(ff_set, 4)
            high1(0, 0, 0)
            high1(0, 0, 1)
            gelu1(0)
            transposed(NT - 1)
            for b in range(1, NB):
                high1(b, b, 0)
                high1(b, b, 1)
            gelu2(0)
            gelu1(1)
            context(0)
            gelu3(0)
            context(1)
            gelu2(1)
            context(2)
            gelu1(2)

            def slot(n, b):
                tanh(n - 3)
                gelu3(n - 2)
                gelu2(n - 1)
                gelu1(n)
                high1(n + 1, (b + 1) % NB, 0)
                high1(n + 1, (b + 1) % NB, 1)

            slot(3, 3)
            with e.Fori(1, CYCLES) as cyc:
                for b in range(NB):
                    slot(cyc * NB + b, b)
            for n in range(CYCLES * NB, CYCLES * NB + 3):
                for late, layer in ((3, tanh), (2, gelu3), (1, gelu2)):
                    if n - late < CYCLES * NB:
                        layer(n - late)

        @block.tensor
        def _(e):
            pe = nc.tensor

            def xt(t_plus, r):
                e.wait_ge(xn_ready, t_plus)
                for half in range(2):
                    last = pe.transpose(bank(TA)[:, C + P * half:C + P * (half + 1)], XN[:, r, P * half:P * (half + 1)], ident[:, :])
                last.then_inc(xt_done, 1)

            def project(dst, m, r, chunks):
                for ck in chunks:
                    k = 0
                    for half in range(2):
                        for xs, ws in ((XH, wh), (XH, wl), (XL, wh)):
                            last = pe.matmul(dst[:, ck, :], xs[:, r, half, :], ws[:, half, m, 512 * ck:512 * (ck + 1)],
                                             start=k == 0, stop=k == 5)
                            k += 1
                return last

            def transposes(src, r, k, done):
                for h in range(8):
                    last = pe.transpose(bank((TB, TA)[k]).bitcast(F16)[:, P * h:P * (h + 1)], src[:, r, 8 * k + h, :], ident16[:, :])
                last.then_inc(done, 1)

            def first_queries(t, r):
                e.wait_ge(q_high, t + 1)
                e.wait_ge(q_low, t + 1)
                transposes(QT, r, 0, trq_done)

            def keys(t, r):
                e.wait_ge(k_high, t + 1)
                e.wait_ge(k_low, t + 1)
                for k in range(2):
                    e.wait_ge(stq_filled, t * 2 + k + 1)
                    transposes(KT, r, k, trk_done)

            def step(t, r, n):
                first, last_t = isinstance(t, int) and t == 0, isinstance(t, int) and t == NT - 1
                e.wait_ge(xh_ready, t + 1)
                e.wait_ge(xl_ready, t + 1)
                if first:
                    e.wait_ge(w_split, 2)
                at_least(e, qn_ready, t)
                project(QB, 0, r, (0, 1)).then_inc(q_done, 1)
                if first:
                    e.wait_ge(w_split, 4)
                at_least(e, kn_ready, t)
                project(KB, 1, r, (0, 1)).then_inc(k_done, 1)
                if first:
                    e.wait_ge(w_split, 6)
                    project(VB, 2, r, (0, 1)).then_inc(v_done, 1)
                    e.wait_ge(w_split, 7)
                at_least(e, stk_filled, t * 2 - 2)
                for k, (half, xs, n) in enumerate(((0, XH, 2), (1, XH, 2), (0, XL, 1), (1, XL, 1))):
                    last = pe.matmul(bank(TA)[:, 0:n * H], xs[:, r, half, :], wg[:, half, 0:n, :].rearrange("p n h -> p (n h)"), start=k == 0, stop=k == 3)
                last.then_inc(g_done, 1)
                if not last_t:
                    xt(t + 2, 1 - r)
                if not first:
                    first_queries(t - 1, 1 - r)
                    at_least(e, v_copied, t)
                    project(VB, 2, r, (0,))
                    e.wait_ge(g_read, t + 1)
                    if not last_t:
                        e.wait_ge(xl_ready, t + 2)
                    transposes(QT, 1 - r, 1, trq_done)
                    project(VB, 2, r, (1,)).then_inc(v_done, 1)
                    keys(t - 1, 1 - r)

            e.wait_ge(consts, 3)
            xt(1, 0)
            tiles(e, step)
            e.wait_ge(stk_filled, 2 * NT - 2)
            first_queries(NT - 1, 1)
            transposes(QT, 1, 1, trq_done)
            keys(NT - 1, 1)
            e.wait_ge(cp_ready, 2)
            for k, tb in enumerate((TA, TB)):
                e.wait_ge(stk_filled, 2 * NT)
                for t in range(8):
                    last = pe.transpose(bank(tb).bitcast(F16)[0:NC * H, P * t:P * (t + 1)],
                                        CP[:, 8 * k + t, :, :].rearrange("p h n -> p (h n)"), ident16[:, :])
                last.then_inc(ct_done, 1)

            def max_unit(m, r):
                b, qt, hd, c, n = max_shape(m)
                dst = mx_bank(m)[:, 0:n]
                q0 = BLK * b + P * qt
                pe.matmul(dst, BM[:, hd, q0:q0 + P], A1[:, r, hd, BLK * c:BLK * c + n], start=True, stop=True).then_inc(mx_done, 1)

            def transpose_rows(n):
                return pe.transpose(bank(MISC)[0:n, 0:P // 2].bitcast(F16), nm[:, 0:n // (2 * TPB), :, :].rearrange("p b h t -> p (b h t)"), ident16[:, :])

            def pv(iv, k):
                par, s_ = divmod(k, NSTEP)
                b, j = STEPS[s_]
                c0 = P * max(j - TPB * b, 0)
                q = iv * 2 + par
                if j == 0:
                    e.wait_ge(o_done, q * NB + (b + 1))
                if j >= TPB * b and j % TPB == 0:
                    e.wait_ge(ld_v[b], q * 16 + 16)
                e.wait_ge(exp_done, iv * (2 * PER_BODY) + (2 * k + 2))
                for hd in range(2):
                    rows = slice(D * hd, D * (hd + 1))
                    last = pe.matmul(o_bank(b)[rows, c0:], V[:, j, rows], PB[:, (2 * k + hd) % P_RING, c0:],
                                     start=j == 0, stop=j == block_tiles(b) - 1)
                last.then_inc(pv_done, 1)

            def misc(i, kind, iv, upar, what):
                e.wait_ge(misc_read, iv * NMISC + (i + 1))
                if kind == "row":
                    e.wait_ge(nm_ready, iv * 6 + (3 * upar + {(2,): 2, (3,): 3, (0, 1): 4}[what]))
                    transpose_rows(2 * TPB * len(what)).then_inc(misc_done, 1)
                else:
                    for hd in range(2):
                        e.wait_ge(sums[hd], iv * PER_BODY + (NSTEP * upar + BLOCK_END[what]))
                        last = pe.matmul(bank(MISC)[D * hd:D * (hd + 1), :], ones[:, :], acc[:, what % 2, hd, :], start=True, stop=True)
                    last.then_inc(misc_done, 1)

            def steps(iv, first, end):
                for k in range(first, end):
                    par, s_ = divmod(k, NSTEP)
                    b, j = STEPS[s_]
                    c0 = P * max(j - TPB * b, 0)
                    q = iv * 2 + par
                    if j == 0:
                        e.wait_ge(ld_b[b], q * 32 + 32)
                        e.wait_ge(mrow_in, q * 128 + {0: 64, 1: 64, 2: 96, 3: 128}[b])
                    if j >= TPB * b and j % TPB == 0:
                        e.wait_ge(ld_a2[b], q * 16 + 16)
                    units = list(max_units(iv, k))
                    for hd in range(2):
                        unit = 2 * k + hd
                        at_least(e, exp_done, iv * (2 * PER_BODY) + (bank_before(unit) + 1))
                        dst = s_bank(unit)[:, c0:]
                        keys, queries = slice(P * j, P * (j + 1)), slice(BLK * b + c0, BLK * (b + 1))
                        pe.matmul(dst, A1[:, par, hd, keys], B1[:, hd, queries], start=True, stop=False)
                        if j >= TPB * b:
                            pe.matmul(dst[:, 0:P], identb[:, :], mask_s[:, :], start=False, stop=False)
                        pe.matmul(dst, A2[:, hd, keys], B2[:, hd, queries], start=False, stop=True).then_inc(s_done, 1)
                        if hd < len(units):
                            at, mpar, m = units[hd]
                            if m == 0:
                                e.wait_ge(ld_a1[mpar], iv * 32 + 32 * (2 if par else 1))
                            if m in BLOCK_STARTS:
                                e.wait_ge(ld_bm[MAXES[m][0]], iv * 32 + 16 * (at // NMAX) + 16)
                            e.wait_ge(mx_read, iv * (2 * NMAX) + (at - 1))
                            max_unit(m, mpar)
                    if not (isinstance(iv, int) and iv == 0 and k < 2):
                        pv(iv, k - 2)
                    for i, kind, upar, what in misc_at(iv, k):
                        misc(i, kind, iv, upar, what)

            e.wait_ge(consts, NCONST)
            e.wait_ge(ct_copied, 2)
            e.wait_ge(ld_a1[0], 32)
            for m in range(LEAD):
                if m in BLOCK_STARTS:
                    e.wait_ge(ld_bm[MAXES[m][0]], 16)
                at_least(e, mx_read, m - 1)
                max_unit(m, 0)
            e.wait_ge(nm_ready, 1)
            transpose_rows(2 * 2 * TPB).then_inc(misc_done, 2)
            bodies(e, steps)
            pv(LAST, PER_BODY - 2)
            pv(LAST, PER_BODY - 1)
            misc(-1, "sums", LAST + 1, -1, NB - 1)
            def stream_transpose(t):
                e.wait_ge(x2_ready, t + 1)
                at_least(e, tt_copied, 2 * t - 2)
                for half in range(2):
                    last = pe.transpose(bank(2 + t % 2)[:, P * half:P * (half + 1)], X2[:, t % 2, P * half:P * (half + 1)], ident[:, :])
                last.then_inc(x2t_done, 1)

            e.wait_ge(wp_split, 2)
            e.wait_ge(att_over, 1)
            for t in range(NT):
                at_least(e, h_added, t - 1)
                e.wait_ge(oh_ready, t + 1)
                e.wait_ge(ol_ready, t + 1)
                for k, (xs, ws) in enumerate(((OH, wph), (OH, wpl), (OL, wph))):
                    for pair in range(NP):
                        last = pe.matmul(bank(t % 2)[:, 0:C], xs[:, t % 2, pair, :], ws[:, pair, :],
                                         start=k == 0 and pair == 0, stop=k == 2 and pair == NP - 1)
                last.then_inc(proj_done, 1)
                if t >= 2:
                    stream_transpose(t - 2)
            stream_transpose(NT - 2)

            def context(i):
                if i == 0:
                    e.wait_ge(gmean_ready, 1)
                    e.wait_ge(h_added, NT)
                    for half in range(2):
                        last = pe.matmul(bank(1)[:, 0:1], gw1[:, half, :], gmean[:, half:half + 1], start=half == 0, stop=half == 1)
                    last.then_inc(g_mm, 1)
                else:
                    e.wait_ge(g_act, i)
                    pe.matmul(bank(1)[:, 0:1], (gw2, gw3)[i - 1][:, :], gv[:, i - 1:i], start=True, stop=True).then_inc(g_mm, 1)

            def layer1(n, b):
                e.wait_ge(th_ready, n * 2 + 2)
                for out_half in range(2):
                    at_least(e, h1h_ready, n * 2 - 1 + out_half)
                    for k, (ws, xs) in enumerate(((w1h, TH), (w1l, TH), (w1h, TL))):
                        for half in range(2):
                            if xs is TL and out_half == 0:
                                e.wait_ge(tl_ready[half], n + 1)
                            last = pe.matmul(bank(4 + out_half), ws[:, half, P * out_half:P * (out_half + 1)], xs[:, half, BLK * b:BLK * (b + 1)],
                                             start=k == 0 and half == 0, stop=k == 2 and half == 1)
                    last.then_inc(l_done[0], 1)

            def layer2(n, b):
                e.wait_ge(h1h_ready, n * 2 + 2)
                at_least(e, a_done[1], n)
                for k, (ws, xs) in enumerate(((w2h, h1h), (w2l, h1h), (w2h, h1l))):
                    for half in range(2):
                        if xs is h1l:
                            e.wait_ge(h1l_ready, n * 2 + half + 1)
                        last = pe.matmul(bank(6), ws[:, half, :], xs[:, half, :], start=k == 0 and half == 0, stop=k == 2 and half == 1)
                last.then_inc(l_done[1], 1)

            def layer3(n, b):
                e.wait_ge(a_done[1], n + 1)
                at_least(e, a_done[2], n)
                pe.matmul(bank(7), w3[:, :], h2[:, :], start=True, stop=True).then_inc(l_done[2], 1)

            def layer4(n, b):
                e.wait_ge(a_done[2], n + 1)
                at_least(e, a_done[3], n)
                pe.matmul(bank(0), w4[:, :], h3[:, :], start=True, stop=True).then_inc(l_done[3], 1)

            def stream_back(b):
                e.wait_ge(t0_new, (CYCLES - 1) * NB + b + 1)
                e.wait_ge(t1_new, (CYCLES - 1) * NB + b + 1)
                for pr in range(2 * b, 2 * b + 2):
                    at_least(e, out_sum, pr - 1)
                    for i in range(2):
                        t = 2 * pr + i
                        for half in range(2):
                            last = pe.transpose(bank(2 + pr % 2)[:, C * i + P * half:C * i + P * (half + 1)], TT[:, half, P * t:P * (t + 1)], ident[:, :])
                    last.then_inc(out_t, 1)

            e.wait_ge(ff_set, 4)
            e.wait_ge(wsplit2, 4)
            layer1(0, 0)
            stream_transpose(NT - 1)
            layer2(0, 0)
            layer1(1, 1)
            context(0)
            layer3(0, 0)
            context(1)
            layer2(1, 1)
            context(2)
            layer1(2, 2)
            for late, layer in ((3, layer4), (2, layer3), (1, layer2), (0, layer1)):
                layer(3 - late, 3 - late)
            with e.Fori(1, CYCLES) as cyc:
                for b in range(NB):
                    for late, layer in ((3, layer4), (2, layer3), (1, layer2), (0, layer1)):
                        layer(cyc * NB + (b - late), (b - late) % NB)
            for n in range(CYCLES * NB, CYCLES * NB + 3):
                for late, layer in ((3, layer4), (2, layer3), (1, layer2)):
                    if n - late < CYCLES * NB:
                        layer(n - late, (n - late) % NB)
                stream_back(n - CYCLES * NB)
            stream_back(NB - 1)

        @block.vector
        def _(e):
            v = nc.vector
            ch = Chain(dv)
            e.wait_ge(ld_ids, 16)
            ch.inc(v.tensor_scalar(far[:, :], ids[:, :], float(NSMALL), FAR, ALU.is_lt, ALU.mult))
            ch.wait(e)
            v.scalar_tensor_tensor(spec_ids[:, :], ids[:, :], -float(NSMALL), far[:, :], ALU.add, ALU.add).then_inc(idx_ready, 1)

            def stats(t, r, n):
                e.wait_ge(tok_in, t * 16 + 16)
                e.wait_ge(spec_in, t * 16 + 16)
                e.wait_ge(small_in[r], n * 16 + 16)
                tile = E[:, bass.ds(t, 1), :].rearrange("p o c -> p (o c)")
                ch.inc(v.bn_stats(bn6[:, r, :], tile))

            def aggregate(r):
                v.bn_aggr(mv[:, r, :], bn6[:, r, :]).then_inc(bn_ready, 1)

            def norm(t, r):
                e.wait_ge(ln_sqrt, t + 1)
                ch.inc(v.reciprocal(lr[:, r, :], ls[:, r, :]))
                ch.wait(e)
                at_least(e, xt_done, t - 1)
                tile = E[:, bass.ds(t, 1), :].rearrange("p o c -> p (o c)")
                v.tensor_scalar(XN[:, r, :], tile, mv[:, r, 0:1], lr[:, r, 0:1], ALU.subtract, ALU.mult).then_inc(xn_ready, 1)

            def split_w(n):
                e.wait_ge(wh_ready, n + 1)
                v.tensor_tensor(wl[:, n % 2, n // 2, :], wst[:, n % WST, :], wh[:, n % 2, n // 2, :].bitcast(F32), ALU.subtract).then_inc(w_split, 1)

            def xt_low(t_plus, r):
                e.wait_ge(xh_ready, t_plus)
                v.tensor_tensor(XL[:, r, :, :].rearrange("p a n -> p (a n)"), bank(TA)[:, C:2 * C],
                                XH[:, r, :, :].rearrange("p a n -> p (a n)").bitcast(F32), ALU.subtract).then_inc(xl_ready, 1)

            e.wait_ge(ld_u, 64)
            ch.inc(v.tensor_tensor(tmp[:, :, :], ub[:, :, :], ub[:, :, :], ALU.mult))
            ch.wait(e)
            v.tensor_reduce(un[:, :], tmp[:, :, :], AX.X, ALU.add).then_inc(u_sq, 1)
            v.tensor_tensor(wqk[:, :], qwb[:, :], kwb[:, :], ALU.mult)
            ch.wait(e)
            ch.inc(v.tensor_tensor(ub[:, :, :], ub[:, :, :], kwb[:, :].rearrange("p (o d) -> p o d", o=1).broadcast_to([P, H, D]), ALU.mult))
            split_w(0)
            split_w(1)
            stats(0, 0, 0)
            ch.wait(e)
            aggregate(0)
            norm(0, 0)
            xt_low(1, 0)
            e.wait_ge(u_norm, 1)
            ch.inc(v.tensor_scalar(un[:, :], un[:, :], U_EPS, float(D) ** 0.5, ALU.max, ALU.mult))
            ch.wait(e)
            ch.inc(v.reciprocal(un[:, :], un[:, :]))
            split_w(2)
            split_w(3)
            stats(1, 1, 0)
            ch.wait(e)
            aggregate(1)
            split_w(4)
            split_w(5)
            for half in range(2):
                ch.wait(e)
                ch.inc(v.tensor_tensor(tmp[:, :, :], wst[:, (2 + half) % WST, :].rearrange("p (h d) -> p h d", d=D), ub[:, :, :], ALU.mult))
                ch.wait(e)
                ch.inc(v.tensor_reduce(wgf[:, half, :], tmp[:, :, :], AX.X, ALU.add))
                ch.wait(e)
                ch.inc(v.tensor_tensor(wgf[:, half, :], wgf[:, half, :], un[:, :], ALU.mult))
            norm(1, 1)
            ch.wait(e)
            ch.inc(v.tensor_copy(wg[:, :, 0, :], wgf[:, :, :]))
            ch.wait(e)
            v.tensor_tensor(wg[:, :, 1, :], wgf[:, :, :], wg[:, :, 0, :].bitcast(F32), ALU.subtract).then_inc(w_split, 1)

            def evac_k(t, r, n):
                for k in range(2):
                    e.wait_ge(trk_done, t * 2 + k + 1)
                    if k == 0 and r == 0:
                        at_least(e, k_stored, n * 16)
                    v.tensor_copy(STK[:, 8 * k:8 * k + 8, P * r:P * (r + 1)],
                                  bank((TB, TA)[k]).bitcast(F16).rearrange("p (h n) -> p h n", n=P)).then_inc(stk_filled, 1)

            def step(t, r, n):
                first, last = isinstance(t, int) and t == 0, isinstance(t, int) and t == NT - 1
                near_end = isinstance(t, int) and t >= NT - 2
                e.wait_ge(sqq_ready, t + 1)
                v.tensor_reduce(ms[:, 0:H], SQ[:, 0:H, :], AX.X, ALU.add).then_inc(redq_done, 1)
                e.wait_ge(sqk_ready, t + 1)
                v.tensor_reduce(ms[:, H:], SQ[:, H:, :], AX.X, ALU.add).then_inc(redk_done, 1)
                if not last:
                    xt_low(t + 2, 1 - r)
                e.wait_ge(g_done, t + 1)
                v.tensor_copy(graw[:, :, :], bank(TA)[:, 0:2 * H].rearrange("p (n h) -> p n h", n=2)).then_inc(g_read, 1)
                if not near_end:
                    stats(t + 2, r, n + 1)
                    ch.wait(e)
                e.wait_ge(sr_ready, t + 1)
                ch.inc(v.reciprocal(rr[:, :], sr[:, :]))
                if not near_end:
                    aggregate(r)
                e.wait_ge(g_read, t + 1)
                ch.wait(e)
                v.tensor_tensor(GP[:, bass.ds(t, 1), :, :].rearrange("p o n h -> p (o n) h"), graw[:, :, :],
                                rr[:, H:2 * H].rearrange("p (o h) -> p o h", o=1).broadcast_to([P, 2, H]), ALU.mult).then_inc(gl_ready, 1)
                for dst, src, k, s in ((QN, QB, 0, qn_ready), (KN, KB, 1, kn_ready)):
                    if k == 1:
                        at_least(e, kw_ready, t)
                    v.tensor_tensor(dst[:, :, :], src.rearrange("p a (h d) -> p (a h) d", d=D),
                                    rr[:, H * k:H * (k + 1)].rearrange("p (h o) -> p h o", o=1).broadcast_to([P, H, D]), ALU.mult).then_inc(s, 1)
                if not near_end:
                    norm(t + 2, r)
                e.wait_ge(q_high, t + 1)
                v.tensor_tensor(QT[:, r, :, 0:D], QN[:, :, :], QT[:, r, :, D:P], ALU.subtract).then_inc(q_low, 1)
                if not first:
                    evac_k(t - 1, 1 - r, n - 1 if r == 0 else n)

            tiles(e, step, 3, ch)
            e.wait_ge(gl_ready, NT)
            e.wait_ge(wp_split, 2)
            ch.inc(v.tensor_tensor(GL[:, 0:NT, :], GP[:, :, 0, :], GP[:, :, 1, :], ALU.add))
            ch.wait(e)
            ch.inc(v.tensor_scalar(na[:, :, :], GL[:, :, :], -1.0, None, ALU.mult))
            ch.wait(e)
            v.tensor_tensor(na[:, :, :], na[:, :, :], GL[:, :, :], ALU.min).then_inc(sp_neg, 1)
            ch.inc(v.tensor_scalar(sp[:, :, :], GL[:, :, :], 0.0, None, ALU.max))
            e.wait_ge(sp_ln, 1)
            ch.wait(e)
            ch.inc(v.tensor_tensor(sp[:, :, :], sp[:, :, :], na[:, :, :], ALU.add))
            ch.wait(e)
            e.wait_ge(consts, NCONST)
            ch.inc(v.tensor_tensor(cw[:, :], sp[:, NT, :], slope[:, :], ALU.mult))
            ch.inc(v.tensor_copy(off[:, :], off_i[:, :]))
            ch.wait(e)
            ch.inc(v.tensor_tensor(cc[:, :, :], sp[:, 0:NT, :], cw[:, :].rearrange("p (o h) -> p o h", o=1).broadcast_to([P, NT, H]), ALU.mult))
            ch.wait(e)
            ch.inc(v.tensor_scalar(rest[:, :, :], cc[:, :, :], -8.0, None, ALU.mult))
            ch.inc(v.tensor_scalar(at_j[:, :], off[:, BIAS_AT[NB - 1]:], float(BLK * (NB - 1)), 0.125, ALU.add, ALU.mult))
            ch.wait(e)
            ch.inc(v.tensor_tensor(jc[:, :, :], cc[:, :, :], at_j[:, :].rearrange("p (t o) -> p t o", o=1).broadcast_to([P, NT, H]), ALU.mult))
            for whole, k, end in ((rest, 0, False), (rest, 1, False), (rest, 2, True), (jc, 3, False), (jc, 4, True)):
                ch.wait(e)
                if end:
                    v.tensor_copy(CP[:, :, :, k], whole[:, :, :]).then_inc(cp_ready, 1)
                else:
                    ch.inc(v.tensor_copy(CP[:, :, :, k], whole[:, :, :]))
                    ch.wait(e)
                    ch.inc(v.tensor_tensor(whole[:, :, :], whole[:, :, :], CP[:, :, :, k], ALU.subtract))
            evac_k(NT - 1, 1, NT // 2 - 1)
            for b in range(NB):
                n, o = block_tiles(b), BIAS_AT[b]
                v.tensor_tensor(BT[:, :, o:o + n], cc[:, 0:n, :].rearrange("p t h -> p h t"),
                                off[:, o:o + n].rearrange("p (o n) -> p o n", o=1).broadcast_to([P, H, n]), ALU.mult).then_inc(bt_ready, 1)

            e.wait_ge(k_stored, 16 * (NT // 2))
            e.wait_ge(v_stored[1], 16 * (NT // 2))
            e.wait_ge(c_stored, 16)
            v.memset(ones[:, :], 1.0).then_inc(o_done, 2)

            def max_read(m, r, count):
                b, qt, hd, c, n = max_shape(m)
                e.wait_ge(mx_done, count)
                if c == b:
                    v.memset(carry[:, m:m + 1], 0.0)
                to, src = mxp[:, r, b, 2 * qt + hd, c:c + 1], mx_bank(m)[:, 0:n]
                if c == b:
                    v.tensor_tensor_reduce(out=src, in0=src, in1=mask_m[:, BLK - n:], scale=1.0, scalar=3 * NEG,
                                           op0=ALU.add, op1=ALU.max, accum_out=to).then_inc(mx_read, 1)
                else:
                    v.tensor_reduce(to, src, AX.X, ALU.max).then_inc(mx_read, 1)

            def negate(r, blocks, reads, links):
                e.wait_ge(mx_read, reads)
                for i, b in enumerate(blocks):
                    v.tensor_reduce(nmf[:, i, :, :].rearrange("p t h -> p (t h)"), mxp[:, r, b, :, 0:b + 1], AX.X, ALU.max).then_inc(dv, 1)
                e.wait_ge(dv, links)
                for i in range(len(blocks)):
                    ins = v.tensor_scalar(nm[:, i, :, :].rearrange("p h t -> p t h"), nmf[:, i, :, :], -0.125, None, ALU.mult)
                ins.then_inc(nm_ready, 1)

            for m in range(LEAD):
                max_read(m, 0, m + 1)
            dv0 = ch.base + ch.n
            negate(0, (0, 1), LEAD, dv0 + 2)

            def output(iv, upar, b):
                q = iv * 2 + upar
                e.wait_ge(r_ready, q * NB + (b + 1))
                v.tensor_tensor(OT[:, bass.ds(q, 1), BLK * b:BLK * (b + 1)].rearrange("p o t -> p (o t)"), o_bank(b), R[:, :], ALU.mult).then_inc(o_done, 1)

            def steps(iv, first, end):
                for k in range(first, end):
                    par, s_ = divmod(k, NSTEP)
                    units = list(max_units(iv, k))
                    for at, mpar, m in units:
                        max_read(m, mpar, iv * (2 * NMAX) + (at + 1))
                    last_pair = isinstance(iv, int) and iv == LAST and par == 1
                    if s_ in T_AT and not (last_pair and T_AT[s_] == (0, 1)):
                        blocks = T_AT[s_]
                        reads = NMAX * par + LEAD + 2 * s_ + 2
                        if last_pair:
                            reads = min(reads, 2 * NMAX)
                        r = 1 - par if blocks == (0, 1) else par
                        rows = [i for i, use in enumerate(MISC_USES) if use[1] == "row" and use[0] <= k]
                        e.wait_ge(misc_done, iv * NMISC + (rows[-1] + 2 if rows else 1))
                        negate(r, blocks, iv * (2 * NMAX) + reads, iv * 8 + (dv0 + 2 + 4 * par + {4: 1, 20: 2, 32: 4}[s_]))
                    if not (isinstance(iv, int) and iv == 0 and k == 0):
                        add_up(e, v, iv, k - 1, 0)
                    if k > 0:
                        for i, kind, upar, what in misc_at(iv, k - 1):
                            if kind == "sums":
                                output(iv, upar, what)

            bodies(e, steps)
            add_up(e, v, LAST, PER_BODY - 1, 0)
            output(LAST, 1, NB - 1)
            fd = Chain(ff_dve)

            def norm2(t):
                e.wait_ge(ln2_sqrt, t + 1)
                fd.inc(v.reciprocal(lrb[:, t % 2, :], lsb[:, t % 2, :]))
                fd.wait(e)
                at_least(e, x2t_done, t - 1)
                v.tensor_scalar(X2[:, t % 2, :], E[:, t, :], mvb[:, t % 2, 0:1], lrb[:, t % 2, :], ALU.subtract, ALU.mult).then_inc(x2_ready, 1)

            def low(t):
                e.wait_ge(oh_ready, t + 1)
                v.tensor_tensor(OL[:, t % 2, :, :], OT[:, :, P * t:P * (t + 1)], OH[:, t % 2, :, :].bitcast(F32), ALU.subtract).then_inc(ol_ready, 1)

            low(0)
            low(1)
            for t in range(NT):
                e.wait_ge(proj_done, t + 1)
                v.tensor_tensor(E[:, t, :], bank(t % 2)[:, 0:C], E[:, t, :], ALU.add).then_inc(h_added, 1)
                e.wait_ge(h_added, t + 1)
                fd.inc(v.bn_stats(bn6b[:, t % 2, :], E[:, t, :]))
                fd.wait(e)
                v.bn_aggr(mvb[:, t % 2, :], bn6b[:, t % 2, :]).then_inc(bn2_ready, 1)
                if t + 2 < NT:
                    low(t + 2)
                if t >= 1:
                    norm2(t - 1)
                if t == NT // 2:
                    e.wait_ge(ld_ff, FF_LOADS * 16)
                    e.wait_ge(ffz, 7)
                    for dst, src in ((w4, w4c), (gw3, gw3c)):
                        v.tensor_copy(dst[0:D, :], src[0:D, :].broadcast_to([D, P])).then_inc(ff_set, 1)
                    v.tensor_scalar(halfb[:, 0:1], bias[:, 4:5], 0.5, None, ALU.mult).then_inc(ff_set, 1)
                    v.tensor_scalar(halfb[:, 1:2], bias[:, 7:8], 0.5, None, ALU.mult).then_inc(ff_set, 1)
            norm2(NT - 1)
            def low0(n, b):
                e.wait_ge(th_ready, n * 2 + 1)
                sl = slice(BLK * b, BLK * (b + 1))
                v.tensor_tensor(TL[:, 0, sl], TT[:, 0, sl], TH[:, 0, sl].bitcast(F32), ALU.subtract).then_inc(tl_ready[0], 1)

            def low_h1(n):
                for half in range(2):
                    e.wait_ge(h1h_ready, n * 2 + half + 1)
                    at_least(e, l_done[1], n)
                    v.tensor_tensor(h1l[:, half, :], h1[:, half, :], h1h[:, half, :].bitcast(F32), ALU.subtract).then_inc(h1l_ready, 1)

            low0(0, 0)
            low_h1(0)
            e.wait_ge(tt_copied, 2 * NT)
            fd.inc(v.tensor_reduce(gmean[:, :], gm[:, :, :], AX.X, ALU.add))
            fd.wait(e)
            v.tensor_scalar(gmean[:, :], gmean[:, :], 1.0 / T, None, ALU.mult).then_inc(gmean_ready, 1)
            low0(1, 1)
            low0(2, 2)
            low0(3, 3)
            low_h1(1)
            fd.inc(v.tensor_scalar(cpl[:, 0:1], bias[:, 8:9], sgn[:, 0:1], 0.3, ALU.mult, ALU.mult))
            e.wait_ge(g_act, 3)
            fd.inc(v.tensor_scalar(gv[:, 3:4], gv[:, 2:3], bias[:, 8:9], 0.7, ALU.mult, ALU.mult))
            fd.wait(e)
            fd.inc(v.tensor_scalar(cpl[:, 1:2], gv[:, 3:4], 0.1, sgn[:, 0:1], ALU.add, ALU.mult))
            fd.wait(e)

            def update(n, b):
                sl = slice(BLK * b, BLK * (b + 1))
                e.wait_ge(a_done[3], n + 1)
                at_least(e, dw_ready, n)
                v.tensor_scalar(cp[:, :], th[:, :], cpl[:, 0:1], cpl[:, 1:2], ALU.mult, ALU.add).then_inc(cp_made, 1)
                e.wait_ge(cp_made, n + 1)
                v.tensor_tensor(du[:, :], cp[:, :], TT[:, 1, sl], ALU.mult).then_inc(du_ready, 1)
                at_least(e, t1_new, n)
                v.tensor_tensor(dw[:, :], cp[:, :], TT[:, 0, sl], ALU.mult).then_inc(dw_ready, 1)
                e.wait_ge(du_ready, n + 1)
                v.tensor_tensor(TT[:, 0, sl], TT[:, 0, sl], du[:, :], ALU.add).then_inc(t0_new, 1)

            def add_back(b):
                for pr in range(2 * b, 2 * b + 2):
                    e.wait_ge(out_t, pr + 1)
                    v.tensor_tensor(E[:, 2 * pr:2 * pr + 2, :].rearrange("p t c -> p (t c)"), bank(2 + pr % 2),
                                    E[:, 2 * pr:2 * pr + 2, :].rearrange("p t c -> p (t c)"), ALU.add).then_inc(out_sum, 1)

            def slot(n, b):
                update(n - 3, (b + 1) % NB)
                low_h1(n)
                low0(n + 1, (b + 1) % NB)

            low_h1(2)
            slot(3, 3)
            with e.Fori(1, CYCLES) as cyc:
                for b in range(NB):
                    slot(cyc * NB + b, b)
            for b in range(1, NB):
                update((CYCLES - 1) * NB + b, b)
                add_back(b - 1)
            add_back(NB - 1)


_INS = ["x", "L0_tok_token_table", "L0_tok_op_table", "L0_tok_var_table", "L0_tok_const_table", "L0_tok_struct_table", "L0_tok_special_table",
        "L0_attn_Wq", "L0_attn_Wk", "L0_attn_Wv", "L0_attn_Wproj", "L0_attn_q_rms_w", "L0_attn_k_rms_w", "L0_attn_omega", "L0_attn_u",
        "L0_ffn_cn_w1", "L0_ffn_cn_b1", "L0_ffn_cn_w2", "L0_ffn_cn_b2", "L0_ffn_cn_w3", "L0_ffn_cn_b3", "L0_ffn_cn_w4", "L0_ffn_cn_b4",
        "L0_ffn_gc_w1", "L0_ffn_gc_b1", "L0_ffn_gc_w2", "L0_ffn_gc_b2", "L0_ffn_gc_w3", "L0_ffn_gc_b3", "L0_ffn_adaptive_range"]


def kernel(**inputs):
    import numpy as _np
    import concourse.bacc as _bacc
    from concourse import mybir as _mybir
    from concourse.bass_utils import run_bass_kernel_spmd as _run

    nc = _bacc.Bacc("TRN2", target_bir_lowering=False, num_devices=1)
    arrays, args = {}, []
    for name in _INS:
        a = _np.ascontiguousarray(inputs[name])
        arrays[f"in_{name}_dram"] = a
        args.append(nc.dram_tensor(f"in_{name}_dram", a.shape, _mybir.dt.from_np(a.dtype), kind="ExternalInput").ap())
    args.append(nc.dram_tensor("out_0_dram", (T, C), F32, kind="ExternalOutput").ap())
    tower(nc, *args)
    r = _run(nc, [arrays], core_ids=[0])
    return r.results[0]["out_0_dram"].reshape(1, T, C)
```
